# Optimizing a Trainium2 kernel written in Bass

```python
import numpy as np
import jax
import jax.numpy as jnp

def _softmax(x, axis=-1):
    return jax.nn.softmax(x, axis=axis)

def _gelu(x):
    return jax.nn.gelu(x, approximate=True)

def _silu(x):
    return jax.nn.silu(x)

def _sigmoid(x):
    return jax.nn.sigmoid(x)

def _layernorm(x, axis=-1, eps=1e-05):
    m = jnp.mean(x, axis=axis, keepdims=True)
    v = jnp.var(x, axis=axis, keepdims=True)
    return (x - m) / jnp.sqrt(v + eps)

def _scatter_add(tgt, idx, src, axis=0):
    return tgt.at[idx].add(src)

def _segment_sum(src, seg, n):
    return jax.ops.segment_sum(src, seg, n)
kernel_name = 'mk_decoder_preln_d1_seqx_r8_a8ec4a'

def setup_inputs(seed: int=0):
    np.random.seed(seed)
    _w = jnp.asarray

    def _rec_inputs():
        import jax
        import jax.numpy as jnp
        _rk = jax.random.key(seed)
        x = -0.0002928 + 1 * jax.random.normal(jax.random.fold_in(_rk, 1), (128, 64, 128), jnp.float32)
        _lenS = 64 - jax.random.randint(jax.random.fold_in(_rk, 7), (128,), 0, max(1, 64 // 4) + 1, jnp.int32)
        _lenS2 = 64 - jax.random.randint(jax.random.fold_in(_rk, 8), (128,), 0, max(1, 64 // 4) + 1, jnp.int32)
        _ctx_1024P = jax.random.normal(jax.random.fold_in(_rk, 11), (128, 16, 128), jnp.float32)
        _ctx_1024c = jax.random.dirichlet(jax.random.fold_in(_rk, 511), 0.3 * jnp.ones((16,), jnp.float32), (128, 64))
        _ctx_1024t = jnp.einsum('bsk,bkd->bsd', _ctx_1024c, _ctx_1024P)
        _ctx_1024t = _ctx_1024t * jax.lax.rsqrt(jnp.mean(jnp.square(_ctx_1024t)) + 1e-12) * 0.953939
        ctx_1024 = -1.39393e-06 + 0.999914 * (_ctx_1024t + 0.3 * jax.random.normal(jax.random.fold_in(_rk, 611), (128, 64, 128), jnp.float32))
        return (x, ctx_1024)
    x, ctx_1024 = _rec_inputs()

    def _L0_attn_setup():
        import jax, jax.numpy as jnp
        import numpy as np
        NUM_HEADS = 16
        HEAD_DIM = 64
        NEG_INF = -1000000000.0

        def rotary_embedding(x, seq_len, head_dim):
            positions = jnp.arange(seq_len)
            dim_pairs = jnp.arange(0, head_dim, 2)
            freqs = 1.0 / 10000.0 ** (dim_pairs / head_dim)
            angles = positions[:, None] * freqs[None, :]
            cos = jnp.cos(angles)[:, None, :]
            sin = jnp.sin(angles)[:, None, :]
            x1 = x[..., ::2]
            x2 = x[..., 1::2]
            out1 = x1 * cos - x2 * sin
            out2 = x1 * sin + x2 * cos
            return jnp.stack([out1, out2], axis=-1).reshape(x.shape)
        key = jax.random.key(seed)
        k1, k2, k3 = jax.random.split(key, 3)
        batch, seq_len, embed_dim = (2, 256, 128)
        x = jax.random.normal(k1, (batch, seq_len, embed_dim), dtype=jnp.float32)
        W_qkv = jax.random.normal(k2, (embed_dim, 3 * NUM_HEADS * HEAD_DIM), dtype=jnp.float32) * 0.02
        W_out = jax.random.normal(k3, (NUM_HEADS * HEAD_DIM, embed_dim), dtype=jnp.float32) * 0.02
        return {'x': x, 'W_qkv': W_qkv, 'W_out': W_out}
    _L0_attn_all = _L0_attn_setup()
    _L0_attn_in = {k: v for k, v in _L0_attn_all.items() if k in ('W_qkv', 'W_out')}
    del _L0_attn_all

    def _L0_xattn_setup():
        import jax, jax.numpy as jnp
        import numpy as np
        DIM = 128
        NUM_HEADS = 16
        HEAD_DIM = DIM // NUM_HEADS
        key = jax.random.key(seed)
        ks = jax.random.split(key, 11)
        B, N, C = (2, 256, DIM)
        s = 1.0 / np.sqrt(C)
        inp = {'q': jax.random.normal(ks[0], (B, N, C), jnp.float32), 'k': jax.random.normal(ks[1], (B, N, C), jnp.float32), 'v': jax.random.normal(ks[2], (B, N, C), jnp.float32), 'Wq': jax.random.normal(ks[3], (C, C), jnp.float32) * s, 'bq': jnp.zeros((C,), jnp.float32), 'Wk': jax.random.normal(ks[4], (C, C), jnp.float32) * s, 'bk': jnp.zeros((C,), jnp.float32), 'Wv': jax.random.normal(ks[5], (C, C), jnp.float32) * s, 'bv': jnp.zeros((C,), jnp.float32), 'Wo': jax.random.normal(ks[6], (C, C), jnp.float32) * s, 'bo': jnp.zeros((C,), jnp.float32)}
        return inp
    _L0_xattn_all = _L0_xattn_setup()
    _L0_xattn_in = {k: v for k, v in _L0_xattn_all.items() if k in ('Wq', 'bq', 'Wk', 'bk', 'Wv', 'bv', 'Wo', 'bo')}
    del _L0_xattn_all

    def _L0_ffn_setup():
        import jax, jax.numpy as jnp
        import numpy as np
        MAX_VAL = 100.0
        key = jax.random.key(seed)
        k1, k2, k3 = jax.random.split(key, 3)
        B, S, D_IN, D_OUT = (4, 1024, 128, 128)
        x = jax.random.normal(k1, (B, S, D_IN), dtype=jnp.float32)
        weights = jax.random.normal(k2, (D_OUT, D_IN), dtype=jnp.float32)
        scale = jnp.ones((D_OUT,), dtype=jnp.float32)
        bias = jax.random.normal(k3, (D_OUT,), dtype=jnp.float32)
        return {'x': x, 'weights': weights, 'scale': scale, 'bias': bias}
    _L0_ffn_all = _L0_ffn_setup()
    _L0_ffn_in = {k: v for k, v in _L0_ffn_all.items() if k in ('weights', 'scale', 'bias')}
    del _L0_ffn_all
    return {'x': x, 'ctx_1024': ctx_1024, 'L0_attn_W_qkv': _L0_attn_in['W_qkv'], 'L0_attn_W_out': _L0_attn_in['W_out'], 'L0_xattn_Wq': _L0_xattn_in['Wq'], 'L0_xattn_bq': _L0_xattn_in['bq'], 'L0_xattn_Wk': _L0_xattn_in['Wk'], 'L0_xattn_bk': _L0_xattn_in['bk'], 'L0_xattn_Wv': _L0_xattn_in['Wv'], 'L0_xattn_bv': _L0_xattn_in['bv'], 'L0_xattn_Wo': _L0_xattn_in['Wo'], 'L0_xattn_bo': _L0_xattn_in['bo'], 'L0_ffn_weights': _L0_ffn_in['weights'], 'L0_ffn_scale': _L0_ffn_in['scale'], 'L0_ffn_bias': _L0_ffn_in['bias']}

def reference(x, ctx_1024, L0_attn_W_qkv, L0_attn_W_out, L0_xattn_Wq, L0_xattn_bq, L0_xattn_Wk, L0_xattn_bk, L0_xattn_Wv, L0_xattn_bv, L0_xattn_Wo, L0_xattn_bo, L0_ffn_weights, L0_ffn_scale, L0_ffn_bias):
    import jax
    import jax.numpy as jnp

    def _L0_attn_ref(x, W_qkv, W_out):
        import jax, jax.numpy as jnp
        import numpy as np
        NUM_HEADS = 16
        HEAD_DIM = 64
        NEG_INF = -1000000000.0

        def rotary_embedding(x, seq_len, head_dim):
            positions = jnp.arange(seq_len)
            dim_pairs = jnp.arange(0, head_dim, 2)
            freqs = 1.0 / 10000.0 ** (dim_pairs / head_dim)
            angles = positions[:, None] * freqs[None, :]
            cos = jnp.cos(angles)[:, None, :]
            sin = jnp.sin(angles)[:, None, :]
            x1 = x[..., ::2]
            x2 = x[..., 1::2]
            out1 = x1 * cos - x2 * sin
            out2 = x1 * sin + x2 * cos
            return jnp.stack([out1, out2], axis=-1).reshape(x.shape)
        batch, seq_len, embed_dim = x.shape
        qkv = jnp.einsum('bse,ef->bsf', x, W_qkv)
        qkv = qkv.reshape(batch, seq_len, 3, NUM_HEADS, HEAD_DIM)
        q, k, v = (qkv[:, :, 0], qkv[:, :, 1], qkv[:, :, 2])
        q = rotary_embedding(q, seq_len, HEAD_DIM)
        k = rotary_embedding(k, seq_len, HEAD_DIM)
        scale = 1.0 / jnp.sqrt(jnp.asarray(HEAD_DIM, dtype=x.dtype))
        scores = jnp.einsum('bqhd,bkhd->bhqk', q, k) * scale
        mask = jnp.tril(jnp.ones((seq_len, seq_len), dtype=bool))[None, None, :, :]
        scores = jnp.where(mask, scores, NEG_INF)
        weights = jax.nn.softmax(scores, axis=-1)
        out = jnp.einsum('bhqk,bkhd->bqhd', weights, v)
        out = out.reshape(batch, seq_len, NUM_HEADS * HEAD_DIM)
        return jnp.einsum('bsf,fe->bse', out, W_out)

    def _L0_xattn_ref(q, k, v, Wq, bq, Wk, bk, Wv, bv, Wo, bo):
        import jax, jax.numpy as jnp
        import numpy as np
        DIM = 128
        NUM_HEADS = 16
        HEAD_DIM = DIM // NUM_HEADS
        B, Nq, C = q.shape
        Nkv = k.shape[1]
        H, D = (NUM_HEADS, HEAD_DIM)
        qh = (q @ Wq.T + bq).reshape(B, Nq, H, D).transpose(0, 2, 1, 3)
        kh = (k @ Wk.T + bk).reshape(B, Nkv, H, D).transpose(0, 2, 1, 3)
        vh = (v @ Wv.T + bv).reshape(B, Nkv, H, D).transpose(0, 2, 1, 3)
        scale = D ** (-0.5)
        attn = jax.nn.softmax(jnp.einsum('bhqd,bhkd->bhqk', qh, kh) * scale, axis=-1)
        out = jnp.einsum('bhqk,bhkd->bhqd', attn, vh)
        out = out.transpose(0, 2, 1, 3).reshape(B, Nq, C)
        return out @ Wo.T + bo

    def _L0_ffn_ref(x, weights, scale, bias):
        import jax, jax.numpy as jnp
        import numpy as np
        MAX_VAL = 100.0
        w = (weights >= 0.0).astype(x.dtype) * 2.0 - 1.0
        y = jnp.einsum('bsi,oi->bso', x, w)
        y = y * scale + bias
        y = jnp.clip(y, -MAX_VAL, MAX_VAL)
        return y
    x = x + _L0_attn_ref(_layernorm(x, axis=-1), L0_attn_W_qkv, L0_attn_W_out)
    x = x + _L0_xattn_ref(_layernorm(x, axis=-1), ctx_1024, ctx_1024, L0_xattn_Wq, L0_xattn_bq, L0_xattn_Wk, L0_xattn_bk, L0_xattn_Wv, L0_xattn_bv, L0_xattn_Wo, L0_xattn_bo)
    x = x + _L0_ffn_ref(_layernorm(x, axis=-1), L0_ffn_weights, L0_ffn_scale, L0_ffn_bias)
    return x

_drawn_inputs = setup_inputs


def setup_inputs(seed=0):
    import zlib

    import numpy as np

    out = dict(_drawn_inputs(seed))
    spreads = {'L0_xattn_bq': (0.0, 0.353),
     'L0_xattn_bk': (0.0, 0.8),
     'L0_xattn_bv': (0.0, 0.1),
     'L0_xattn_bo': (0.0, 0.1),
     'L0_ffn_scale': (1.0, 0.2)}
    factors = {}
    for name, (base, spread) in spreads.items():
        noise = np.random.default_rng([zlib.crc32(name.encode()), seed]).standard_normal(out[name].shape)
        drawn = base * np.exp(spread * noise) if base else spread * noise
        out[name] = jnp.asarray(drawn.astype(out[name].dtype))
    for name, factor in factors.items():
        out[name] = (out[name] * factor).astype(out[name].dtype)
    return out
```

```python
from contextlib import ExitStack

import numpy as np

import concourse.bass as bass
from concourse import mybir

F32 = mybir.dt.float32
F32R = mybir.dt.float32r
BF16 = mybir.dt.bfloat16
ALU = mybir.AluOpType
ACT = mybir.ActivationFunctionType
AX_X = mybir.AxisListType.X

P = 128
D = 128
SEQ = 64
NB = P // SEQ
H = 16
PAIRS = H // 2
HD = 64
CHD = D // H
F = H * HD
BANK = 512
GROUP = 4
EPS = 1e-5
CLIP = 100.0
MASKED = -1e30


def decoder_layer(nc, x, ctx_in, w_q, w_k, w_v, w_o, c_wq, c_wk, c_wv, c_wo, c_bq, c_bk, c_bv,
                  c_bo, f_w, f_scale, f_bias, ident_in, mask_in, rope_in, group_in, out):
    NT = x.shape[0] // P
    FIRST_STEP, LAST_STEP = -1, NT + 2
    LOOP_FROM, LOOP_TO = 6, NT - 2

    with ExitStack() as ctx:
        def sb(name, shape, dt=F32):
            return ctx.enter_context(nc.sbuf_tensor(name, shape, dt))

        def sem(name):
            return ctx.enter_context(nc.semaphore(name))

        slot = [ctx.enter_context(nc.psum_tensor(f"slot{i}", [P, 2 * BANK], F32)) for i in range(3)]
        bank = [ctx.enter_context(nc.psum_tensor(f"bank{i}", [P, BANK], F32)) for i in range(2)]

        w_qk = [sb(f"w_qk{i}", [P, F]) for i in range(2)]
        w_qk_hi = [sb(f"w_qk_hi{i}", [P, F], F32R) for i in range(2)]
        w_qk_lo = [sb(f"w_qk_lo{i}", [P, F], F32R) for i in range(2)]
        wv = sb("wv", [P, 2, F // 2])
        wo = sb("wo", [P, PAIRS, D])
        cwq = sb("cwq", [P, D])
        cwk = sb("cwk", [P, D])
        cwv = sb("cwv", [P, 2, D // 2])
        cwo = sb("cwo", [P, D])
        cbq = sb("cbq", [P, 1])
        cbk = sb("cbk", [P, 1])
        cbv = sb("cbv", [P, D // 2])
        cbo = sb("cbo", [P, D])
        fw_raw = sb("fw_raw", [P, D])
        fw = sb("fw", [P, D])
        fscale = sb("fscale", [P, D])
        fbias = sb("fbias", [P, D])
        ident = sb("ident", [P, P])
        ident_b = sb("ident_b", [P, P], BF16)
        mask_f = sb("mask_f", [P, BANK])
        mask_b = sb("mask_b", [P, BANK], BF16)
        rope_c = sb("rope_c", [P, HD])
        rope_s = sb("rope_s", [P, HD])
        gmask = sb("gmask", [P, GROUP])
        jmask = sb("jmask", [P, GROUP])
        neg_half = sb("neg_half", [P, 1])
        eps = sb("eps", [P, 1])
        zero = sb("zero", [P, 1])
        after_stats = sb("after_stats", [P, 1])

        x_in = [sb(f"x_in{i}", [P, D]) for i in range(2)]
        c_in = [sb(f"c_in{i}", [P, D]) for i in range(2)]
        x_res = [sb(f"x_res{i}", [P, D]) for i in range(2)]
        stats = [sb(f"stats{i}", [P, 6]) for i in range(3)]
        mv = [sb(f"mv{i}", [P, 2]) for i in range(3)]
        veps = [sb(f"veps{i}", [P, 1]) for i in range(3)]
        rstd = [sb(f"rstd{i}", [P, 1]) for i in range(3)]
        centred = [sb(f"centred{i}", [P, D]) for i in range(3)]
        xn = sb("xn", [P, D])
        xnT = sb("xnT", [P, P])
        xnT_hi = sb("xnT_hi", [P, P], F32R)
        xnT_lo = sb("xnT_lo", [P, P], F32R)
        q_cos = sb("q_cos", [P, F])
        q_sin = sb("q_sin", [P, F])
        k_cos = sb("k_cos", [P, F])
        k_sin = sb("k_sin", [P, F])
        q_rot = sb("q_rot", [P, F])
        k_rot = sb("k_rot", [P, F])
        qT = sb("qT", [P, PAIRS, P])
        k_bd = sb("k_bd", [P, PAIRS, NB, 2, SEQ])
        v_bd = [sb(f"v_bd{i}", [P, NB, PAIRS, 2, HD]) for i in range(2)]
        probs = sb("probs", [P, H, SEQ])
        pmax = sb("pmax", [P, H])
        psum_ = sb("psum_", [P, H])
        pinv = sb("pinv", [P, H])
        pT = sb("pT", [P, PAIRS, P])
        o = sb("o", [P, F])
        oT = sb("oT", [P, PAIRS, P])
        x1 = sb("x1", [P, D])
        x1_bo = [sb(f"x1_bo{i}", [P, D]) for i in range(2)]
        x1n = sb("x1n", [P, D])
        x1nT = sb("x1nT", [P, P])
        ctxT = sb("ctxT", [P, P])
        cq_g = sb("cq_g", [P, GROUP, P])
        ck_j = sb("ck_j", [P, GROUP, P])
        cv_bd = sb("cv_bd", [P, NB, PAIRS * D])
        cprobs = sb("cprobs", [P, H, SEQ])
        cmax = sb("cmax", [P, H])
        csum = sb("csum", [P, H])
        cinv = sb("cinv", [P, H])
        cpT = sb("cpT", [P, PAIRS, P])
        co = sb("co", [P, D])
        coT = sb("coT", [P, P])
        x2 = sb("x2", [P, D])
        x2n = sb("x2n", [P, D])
        x2nT = sb("x2nT", [P, P])
        f_scaled = sb("f_scaled", [P, D])
        f_biased = sb("f_biased", [P, D])
        f_clipped = sb("f_clipped", [P, D])
        y = [sb(f"y{i}", [P, D]) for i in range(2)]

        weights_in = sem("weights_in")
        x_loaded = [sem(f"x_loaded{i}") for i in range(2)]
        ctx_loaded = [sem(f"ctx_loaded{i}") for i in range(2)]
        y_stored = [sem(f"y_stored{i}") for i in range(2)]
        act_setup, dve_setup, pool_setup, fw_doubled = map(sem, ["act_setup", "dve_setup", "pool_setup", "fw_doubled"])
        t_xT, t_q, t_k, t_v, t_qT, t_kT = map(sem, ["t_xT", "t_q", "t_k", "t_v", "t_qT", "t_kT"])
        t_s, t_pT, t_o, t_oT, t_out = map(sem, ["t_s", "t_pT", "t_o", "t_oT", "t_out"])
        t_x1T, t_cq, t_ctxT, t_ck, t_cv = map(sem, ["t_x1T", "t_cq", "t_ctxT", "t_ck", "t_cv"])
        t_cs, t_cpT, t_co, t_coT, t_cout = map(sem, ["t_cs", "t_cpT", "t_co", "t_coT", "t_cout"])
        t_x2T, t_ffn = map(sem, ["t_x2T", "t_ffn"])
        a_xT, a_v, a_qT, a_k, a_exp = map(sem, ["a_xT", "a_v", "a_qT", "a_k", "a_exp"])
        a_pT, a_oT, a_x1T, a_ctxT, a_cexp = map(sem, ["a_pT", "a_oT", "a_x1T", "a_ctxT", "a_cexp"])
        a_cpT, a_coT, a_x2T = map(sem, ["a_cpT", "a_coT", "a_x2T"])
        d_stats = [sem(f"d_stats{i}") for i in range(3)]
        d_mv = [sem(f"d_mv{i}") for i in range(3)]
        d_xlo, d_q, d_k, d_max, d_sub, d_sum, d_inv, d_o, d_x1 = map(
            sem, ["d_xlo", "d_q", "d_k", "d_max", "d_sub", "d_sum", "d_inv", "d_o", "d_x1"])
        d_cq, d_ck, d_cv, d_cmax, d_csub, d_csum, d_cinv, d_co, d_x2 = map(
            sem, ["d_cq", "d_ck", "d_cv", "d_cmax", "d_csub", "d_csum", "d_cinv", "d_co", "d_x2"])
        d_ffn, d_clipped = map(sem, ["d_ffn", "d_clipped"])
        g_veps = [sem(f"g_veps{i}") for i in range(3)]
        g_rstd = [sem(f"g_rstd{i}") for i in range(3)]
        g_xn, g_x1n, g_x2n, g_xres, g_q, g_k, g_x1bo, g_biased, g_y = map(
            sem, ["g_xn", "g_x1n", "g_x2n", "g_xres", "g_q", "g_k", "g_x1bo", "g_biased", "g_y"])

        class Tile:

            def __init__(self, base, off):
                self.base, self.off = base, off
                self.looped = not isinstance(base, int)
                self.n = base + off
                self.par = (off if self.looped else base + off) % 2
                self.landed = (self.n - self.par) * 8 + 16

            def exists(self, before=0):
                return self.looped or 0 <= self.n - before < NT

        class Step:

            def __init__(self, base, off=0):
                self.base, self.off = base, off

            def tile(self, phase):
                return Tile(self.base, self.off + 1 - phase)

        def run(eng, body):
            for s in range(FIRST_STEP, LOOP_FROM):
                body(Step(s))
            with eng.Fori(LOOP_FROM, LOOP_TO - 1, 2) as s:
                body(Step(s, 0))
                body(Step(s, 1))
            for s in range(LOOP_TO, LAST_STEP + 1):
                body(Step(s))

        SCORES, C_SCORES, C_PROBS_T, O_T = range(4)
        in_slot0 = [(2, d_sub), (3, d_csub), (3, a_cpT), (2, a_oT)]
        V, PROBS_T, ATTEND, K_T = range(4)
        in_slot1 = [(1, a_v), (2, a_pT), (2, d_o), (1, a_k)]
        Q, K, Q_T = range(3)
        in_slot2 = [(1, d_q), (1, d_k), (1, a_qT)]
        C_K, X1_T, X2_T, X_T, CTX_T, CO_T = range(6)
        in_bank0 = [(3, d_ck), (3, a_x1T), (4, a_x2T), (0, d_xlo), (2, a_ctxT), (3, a_coT)]
        C_V, C_Q, FFN, C_ATTEND, OUT, C_OUT = range(6)
        in_bank1 = [(3, d_cv), (3, d_cq), (4, d_ffn), (3, d_co), (2, d_x1), (3, d_x2)]

        def read_out(held, me, s):
            for back in range(1, 4 * len(held)):
                phase, read = held[(me - back) % len(held)]
                tile = Tile(s.base, s.off + 1 - phase - (len(held) - 1 - me + back) // len(held))
                if tile.exists():
                    return read, tile.n + 1
            return pool_setup, 1

        load_list = [
            (w_qk[0][:], w_q), (w_qk[1][:], w_k), (wv[:], w_v), (wo[:], w_o), (cwq[:], c_wq), (cwk[:], c_wk),
            (cwv[:], c_wv), (cwo[:], c_wo), (cbq[:], c_bq), (cbk[:], c_bk),
            (cbv[0:SEQ], c_bv[0:1, :].broadcast_to([SEQ, D // 2])),
            (cbv[SEQ:P], c_bv[1:2, :].broadcast_to([SEQ, D // 2])),
            (cbo[:], c_bo.broadcast_to([P, D])), (fw_raw[:], f_w),
            (fscale[:], f_scale.broadcast_to([P, D])), (fbias[:], f_bias.broadcast_to([P, D])),
            (ident[:], ident_in), (mask_f[:], mask_in), (rope_c[:], rope_in[0]), (rope_s[:], rope_in[1]),
            (gmask[:], group_in[0]), (jmask[:], group_in[1]),
        ]
        ALL_WEIGHTS = 16 * len(load_list)

        def halves(a):
            return [a[:, i * BANK:(i + 1) * BANK] for i in range(F // BANK)]

        def squares(a):
            return [a[:, i * P:(i + 1) * P] for i in range(F // P)]

        def seq(b):
            return slice(b * SEQ, (b + 1) * SEQ)

        block = ctx.enter_context(nc.Block())

        @block.sync
        def _(sp):
            def load_x(t):
                if t.exists():
                    if t.exists(2):
                        sp.wait_ge(g_xres, t.n - 1)
                        sp.wait_ge(g_xn, t.n - 1)
                    sp.dma_start(x_in[t.par][:], x[bass.ds(t.n * P, P), :]).then_inc(x_loaded[t.par], 16)

            load_x(Tile(0, 0))
            for dst, src in load_list:
                sp.dma_start(dst, src).then_inc(weights_in, 16)

            def step(s):
                t = s.tile(1)
                if t.exists():
                    if t.exists(2):
                        sp.wait_ge(t_ctxT, t.n - 1)
                    sp.dma_start(c_in[t.par][:], ctx_in[bass.ds(t.n * P, P), :]).then_inc(ctx_loaded[t.par], 16)
                load_x(Tile(s.base, s.off + 2))
                t = s.tile(4)
                if t.exists():
                    sp.wait_ge(g_y, t.n + 1)
                    sp.dma_start(out[bass.ds(t.n * P, P), :], y[t.par][:]).then_inc(y_stored[t.par], 16)

            run(sp, step)
            for t in (Tile(NT - 2, 0), Tile(NT - 1, 0)):
                sp.wait_ge(y_stored[t.par], t.landed)

        @block.tensor
        def _(pe):
            mm, transpose = nc.tensor.matmul, nc.tensor.transpose
            pe.wait_ge(weights_in, ALL_WEIGHTS)
            pe.wait_ge(dve_setup, 1)
            pe.wait_ge(pool_setup, 1)

            def context_kv(t, s):
                pe.wait_ge(a_ctxT, t.n + 1)
                pe.wait_ge(*read_out(in_bank0, C_K, s))
                mm(bank[0][:, 0:P], cwk[:], ctxT[:], start=True, stop=True).then_inc(t_ck, 1)
                pe.wait_ge(*read_out(in_bank1, C_V, s))
                for b in range(NB):
                    for par in range(2):
                        last = mm(bank[1][seq(par), b * (D // 2):(b + 1) * (D // 2)], ctxT[:, seq(b)],
                                  cwv[:, par, :], start=True, stop=True, skip_group_check=True)
                last.then_inc(t_cv, 1)

            def scores(t, s):
                pe.wait_ge(*read_out(in_slot0, SCORES, s))
                pe.wait_ge(a_qT, t.n + 1)
                pe.wait_ge(a_k, t.n + 1)
                for half, cols in enumerate(halves(slot[0])):
                    mm(cols, ident_b[:], mask_b[:], start=True, stop=False, skip_group_check=True)
                    for pair in range(half * PAIRS // 2, (half + 1) * PAIRS // 2):
                        for b in range(NB):
                            last = mm(slot[0][seq(b), pair * P:(pair + 1) * P], qT[:, pair, seq(b)],
                                      k_bd[:, pair, b, :, :].rearrange("p a k -> p (a k)"),
                                      start=False, stop=True, skip_group_check=True)
                last.then_inc(t_s, 1)

            def v_proj(t, s):
                pe.wait_ge(*read_out(in_slot1, V, s))
                pe.wait_ge(a_xT, t.n + 1)
                for b, cols in enumerate(halves(slot[1])):
                    for par in range(2):
                        last = mm(cols[seq(par), :], xnT[:, seq(b)], wv[:, par, :], start=True, stop=True,
                                  skip_group_check=True)
                last.then_inc(t_v, 1)

            def qk_proj(which):
                hi, lo = halves(w_qk_hi[which]), halves(w_qk_lo[which])
                for cols, w_hi, w_lo in zip(halves(slot[2]), hi, lo):
                    mm(cols, xnT_hi[:], w_hi, start=True, stop=False)
                    mm(cols, xnT_hi[:], w_lo, start=False, stop=False)
                    last = mm(cols, xnT_lo[:], w_hi, start=False, stop=True)
                return last

            def cross_scores(t, s):
                pe.wait_ge(*read_out(in_slot0, C_SCORES, s))
                pe.wait_ge(d_ck, t.n + 1)
                pe.wait_ge(d_cq, t.n + 1)
                width = GROUP * SEQ
                for g in range(GROUP):
                    for b in range(NB):
                        last = mm(slot[0][seq(b), g * width:(g + 1) * width], cq_g[:, g, seq(b)],
                                  ck_j[:, :, seq(b)], start=True, stop=True, skip_group_check=True)
                last.then_inc(t_cs, 1)

            def attend(t, s):
                pe.wait_ge(*read_out(in_slot1, ATTEND, s))
                pe.wait_ge(a_v, t.n + 1)
                pe.wait_ge(a_pT, t.n + 1)
                for pair in range(PAIRS):
                    for b in range(NB):
                        last = mm(slot[1][seq(b), pair * P:(pair + 1) * P], pT[:, pair, seq(b)],
                                  v_bd[t.par][:, b, pair, :, :].rearrange("p a k -> p (a k)"),
                                  start=True, stop=True, skip_group_check=True)
                last.then_inc(t_o, 1)

            def cross_attend(t, s):
                pe.wait_ge(*read_out(in_bank1, C_ATTEND, s))
                pe.wait_ge(d_cv, t.n + 1)
                pe.wait_ge(a_cpT, t.n + 1)
                for pair in range(PAIRS):
                    for b in range(NB):
                        last = mm(bank[1][seq(b), 0:D], cpT[:, pair, seq(b)], cv_bd[:, b, pair * D:(pair + 1) * D],
                                  start=pair == 0, stop=pair == PAIRS - 1, skip_group_check=True)
                last.then_inc(t_co, 1)

            def step(s):
                t0, t1, t2, t3, t4 = (s.tile(phase) for phase in range(5))
                if t3.exists():
                    context_kv(t3, s)
                if t2.exists():
                    scores(t2, s)
                if t3.exists():
                    pe.wait_ge(*read_out(in_bank0, X1_T, s))
                    pe.wait_ge(g_x1n, t3.n + 1)
                    transpose(bank[0][:, 0:P], x1n[:], ident[:]).then_inc(t_x1T, 1)
                if t1.exists():
                    v_proj(t1, s)
                if t3.exists():
                    pe.wait_ge(*read_out(in_bank1, C_Q, s))
                    pe.wait_ge(a_x1T, t3.n + 1)
                    mm(bank[1][:, 0:P], cwq[:], x1nT[:], start=True, stop=True).then_inc(t_cq, 1)
                if t4.exists():
                    pe.wait_ge(*read_out(in_bank0, X2_T, s))
                    pe.wait_ge(g_x2n, t4.n + 1)
                    transpose(bank[0][:, 0:P], x2n[:], ident[:]).then_inc(t_x2T, 1)
                if t1.exists():
                    pe.wait_ge(*read_out(in_slot2, Q, s))
                    pe.wait_ge(d_xlo, t1.n + 1)
                    qk_proj(0).then_inc(t_q, 1)
                if t3.exists():
                    cross_scores(t3, s)
                if t4.exists():
                    pe.wait_ge(*read_out(in_bank1, FFN, s))
                    pe.wait_ge(a_x2T, t4.n + 1)
                    mm(bank[1][:, 0:D], x2nT[:], fw[:], start=True, stop=True).then_inc(t_ffn, 1)
                if t2.exists():
                    pe.wait_ge(*read_out(in_slot1, PROBS_T, s))
                    pe.wait_ge(a_exp, t2.n + 1)
                    for dst, src in zip(squares(slot[1]), squares(probs[:].rearrange("p h k -> p (h k)"))):
                        last = transpose(dst, src, ident[:])
                    last.then_inc(t_pT, 1)
                if t1.exists():
                    pe.wait_ge(*read_out(in_slot2, K, s))
                    qk_proj(1).then_inc(t_k, 1)
                if t2.exists():
                    attend(t2, s)
                if t3.exists():
                    pe.wait_ge(*read_out(in_slot0, C_PROBS_T, s))
                    pe.wait_ge(a_cexp, t3.n + 1)
                    for dst, src in zip(squares(slot[0]), squares(cprobs[:].rearrange("p h k -> p (h k)"))):
                        last = transpose(dst, src, ident[:])
                    last.then_inc(t_cpT, 1)
                if t0.exists():
                    pe.wait_ge(*read_out(in_bank0, X_T, s))
                    pe.wait_ge(g_xn, t0.n + 1)
                    transpose(bank[0][:, 0:P], xn[:], ident[:]).then_inc(t_xT, 1)
                if t1.exists():
                    pe.wait_ge(*read_out(in_slot2, Q_T, s))
                    pe.wait_ge(g_q, t1.n + 1)
                    for dst, src in zip(squares(slot[2]), squares(q_rot)):
                        last = transpose(dst, src, ident[:])
                    last.then_inc(t_qT, 1)
                if t3.exists():
                    cross_attend(t3, s)
                if t2.exists():
                    pe.wait_ge(*read_out(in_slot0, O_T, s))
                    pe.wait_ge(d_o, t2.n + 1)
                    for dst, src in zip(squares(slot[0]), squares(o)):
                        last = transpose(dst, src, ident[:])
                    last.then_inc(t_oT, 1)
                if t2.exists():
                    pe.wait_ge(*read_out(in_bank0, CTX_T, s))
                    pe.wait_ge(ctx_loaded[t2.par], t2.landed)
                    transpose(bank[0][:, 0:P], c_in[t2.par][:], ident[:]).then_inc(t_ctxT, 1)
                if t1.exists():
                    pe.wait_ge(*read_out(in_slot1, K_T, s))
                    pe.wait_ge(g_k, t1.n + 1)
                    for dst, src in zip(squares(slot[1]), squares(k_rot)):
                        last = transpose(dst, src, ident[:])
                    last.then_inc(t_kT, 1)
                if t3.exists():
                    pe.wait_ge(*read_out(in_bank0, CO_T, s))
                    pe.wait_ge(d_co, t3.n + 1)
                    transpose(bank[0][:, 0:P], co[:], ident[:]).then_inc(t_coT, 1)
                if t2.exists():
                    pe.wait_ge(*read_out(in_bank1, OUT, s))
                    pe.wait_ge(a_oT, t2.n + 1)
                    for pair in range(PAIRS):
                        last = mm(bank[1][:, 0:D], oT[:, pair, :], wo[:, pair, :],
                                  start=pair == 0, stop=pair == PAIRS - 1)
                    last.then_inc(t_out, 1)
                if t3.exists():
                    pe.wait_ge(*read_out(in_bank1, C_OUT, s))
                    pe.wait_ge(a_coT, t3.n + 1)
                    mm(bank[1][:, 0:D], coT[:], cwo[:], start=True, stop=True).then_inc(t_cout, 1)

            run(pe, step)

        @block.scalar
        def _(act):
            copy = nc.scalar.copy
            act.wait_ge(weights_in, ALL_WEIGHTS)
            for i in range(2):
                last = copy(w_qk_hi[i][:], w_qk[i][:])
            last.then_inc(act_setup, 1)
            act.wait_ge(pool_setup, 1)

            def wide(a):
                return a[:].rearrange("p r t -> p (r t)")

            def step(s):
                t0, t1, t2, t3, t4 = (s.tile(phase) for phase in range(5))
                if t3.exists():
                    act.wait_ge(t_x1T, t3.n + 1)
                    if t3.exists(1):
                        act.wait_ge(t_cq, t3.n)
                    copy(x1nT[:], bank[0][:, 0:P]).then_inc(a_x1T, 1)
                if t2.exists():
                    act.wait_ge(d_sub, t2.n + 1)
                    nc.scalar.activation(probs[:], probs[:], ACT.Exp, scale=float(HD) ** -0.5).then_inc(a_exp, 1)
                if t1.exists():
                    act.wait_ge(t_v, t1.n + 1)
                    if t1.exists(2):
                        act.wait_ge(t_o, t1.n - 1)
                    for par in range(2):
                        last = copy(v_bd[t1.par][seq(par), :, :, par, :].rearrange("p b r d -> p (b r) d"),
                                    slot[1][seq(par), :].rearrange("p (r d) -> p r d", d=HD))
                    last.then_inc(a_v, 1)
                if t4.exists():
                    act.wait_ge(t_x2T, t4.n + 1)
                    if t4.exists(1):
                        act.wait_ge(t_ffn, t4.n)
                    copy(x2nT[:], bank[0][:, 0:P]).then_inc(a_x2T, 1)
                if t2.exists():
                    act.wait_ge(t_pT, t2.n + 1)
                    if t2.exists(1):
                        act.wait_ge(t_o, t2.n)
                    copy(wide(pT), slot[1][:]).then_inc(a_pT, 1)
                if t3.exists():
                    act.wait_ge(d_csub, t3.n + 1)
                    nc.scalar.activation(cprobs[:], cprobs[:], ACT.Exp, scale=float(CHD) ** -0.5).then_inc(a_cexp, 1)
                if t3.exists():
                    act.wait_ge(t_cpT, t3.n + 1)
                    if t3.exists(1):
                        act.wait_ge(t_co, t3.n)
                    copy(wide(cpT), slot[0][:]).then_inc(a_cpT, 1)
                if t0.exists():
                    act.wait_ge(t_xT, t0.n + 1)
                    if t0.exists(1):
                        act.wait_ge(t_k, t0.n)
                    copy(xnT[:], bank[0][:, 0:P])
                    copy(xnT_hi[:], bank[0][:, 0:P]).then_inc(a_xT, 1)
                if t1.exists():
                    act.wait_ge(t_qT, t1.n + 1)
                    if t1.exists(1):
                        act.wait_ge(t_s, t1.n)
                    copy(wide(qT), slot[2][:]).then_inc(a_qT, 1)
                if t2.exists():
                    act.wait_ge(t_oT, t2.n + 1)
                    if t2.exists(1):
                        act.wait_ge(t_out, t2.n)
                    copy(wide(oT), slot[0][:]).then_inc(a_oT, 1)
                if t2.exists():
                    act.wait_ge(t_ctxT, t2.n + 1)
                    if t2.exists(1):
                        act.wait_ge(t_cv, t2.n)
                    copy(ctxT[:], bank[0][:, 0:P]).then_inc(a_ctxT, 1)
                if t3.exists():
                    act.wait_ge(t_coT, t3.n + 1)
                    if t3.exists(1):
                        act.wait_ge(t_cout, t3.n)
                    copy(coT[:], bank[0][:, 0:P]).then_inc(a_coT, 1)
                if t1.exists():
                    act.wait_ge(t_kT, t1.n + 1)
                    if t1.exists(1):
                        act.wait_ge(t_s, t1.n)
                    for par in range(2):
                        last = copy(k_bd[seq(par), :, :, par, :].rearrange("p r b k -> p (r b) k"),
                                    slot[1][seq(par), :].rearrange("p (r k) -> p r k", k=SEQ))
                    last.then_inc(a_k, 1)

            run(act, step)

        @block.vector
        def _(dve):
            tt = nc.vector.tensor_tensor
            dve.wait_ge(weights_in, ALL_WEIGHTS)
            dve.wait_ge(pool_setup, 1)
            nc.vector.tensor_copy(ident_b[:], ident[:])
            nc.vector.tensor_copy(mask_b[:], mask_f[:])
            nc.vector.tensor_scalar(fw[:], fw_raw[:], 0.0, 2.0, ALU.is_ge, ALU.mult).then_inc(fw_doubled, 1)
            dve.wait_ge(fw_doubled, 1)
            nc.vector.tensor_scalar(fw[:], fw[:], 1.0, None, ALU.subtract)
            dve.wait_ge(act_setup, 1)
            for i in range(2):
                last = tt(w_qk_lo[i][:], w_qk[i][:], w_qk_hi[i][:].bitcast(F32), ALU.subtract)
            last.then_inc(dve_setup, 1)

            def mean_and_variance(t, k, src):
                nc.vector.bn_stats(stats[k][:], src).then_inc(d_stats[k], 1)
                dve.wait_ge(d_stats[k], t.n + 1)
                tt(after_stats[:], eps[:], eps[:], ALU.add)
                nc.vector.bn_aggr(mv[k][:], stats[k][:]).then_inc(d_mv[k], 1)

            def by_head(a, width):
                return a.rearrange("p (h d) -> p h d", d=width)

            def for_heads(a, width):
                return a[:].unsqueeze(2).broadcast_to([P, H, width])

            def rope_products(q_or_k, with_cos, with_sin):
                v = by_head(q_or_k, HD)
                tt(by_head(with_cos[:], HD), v, rope_c[:].unsqueeze(1).broadcast_to([P, H, HD]), ALU.mult)
                return tt(by_head(with_sin[:], HD), v, rope_s[:].unsqueeze(1).broadcast_to([P, H, HD]), ALU.mult)

            def masked_rows(dst, src, bias, masks):
                return nc.vector.scalar_tensor_tensor(
                    out=dst[:], in0=src.unsqueeze(1).broadcast_to([P, GROUP, P]), scalar=bias[:],
                    in1=masks[:].unsqueeze(2).broadcast_to([P, GROUP, P]), op0=ALU.add, op1=ALU.mult)

            def diagonal(blocks, start):
                first = blocks[:, start:start + CHD]
                return bass.AP(first.tensor, first.offset, [first.ap[0], [D + 2 * CHD, PAIRS], [1, CHD]])

            def step(s):
                t0, t1, t2, t3, t4 = (s.tile(phase) for phase in range(5))
                if t3.exists():
                    dve.wait_ge(t_ck, t3.n + 1)
                    if t3.exists(1):
                        dve.wait_ge(t_cs, t3.n)
                    masked_rows(ck_j, bank[0][:, 0:P], cbk, jmask).then_inc(d_ck, 1)
                    dve.wait_ge(t_cv, t3.n + 1)
                    if t3.exists(1):
                        dve.wait_ge(t_co, t3.n)
                    for par in range(2):
                        for b in range(NB):
                            v = bank[1][seq(par), b * (D // 2):(b + 1) * (D // 2)]
                            last = tt(diagonal(cv_bd[seq(par), b, :], par * CHD), by_head(v, CHD),
                                      by_head(cbv[seq(par), :], CHD), ALU.add)
                    last.then_inc(d_cv, 1)
                if t0.exists():
                    dve.wait_ge(x_loaded[t0.par], t0.landed)
                    if t0.exists(1):
                        dve.wait_ge(g_xn, t0.n)
                    mean_and_variance(t0, 0, x_in[t0.par][:])
                if t2.exists():
                    dve.wait_ge(t_s, t2.n + 1)
                    nc.vector.tensor_reduce(pmax[:], by_head(slot[0][:], SEQ), AX_X, ALU.max).then_inc(d_max, 1)
                    dve.wait_ge(d_max, t2.n + 1)
                    if t2.exists(1):
                        dve.wait_ge(t_pT, t2.n)
                    tt(probs[:], by_head(slot[0][:], SEQ), for_heads(pmax, SEQ), ALU.subtract).then_inc(d_sub, 1)
                if t3.exists():
                    dve.wait_ge(t_cq, t3.n + 1)
                    if t3.exists(1):
                        dve.wait_ge(t_cs, t3.n)
                    masked_rows(cq_g, bank[1][:, 0:P], cbq, gmask).then_inc(d_cq, 1)
                if t1.exists():
                    dve.wait_ge(t_q, t1.n + 1)
                    if t1.exists(1):
                        dve.wait_ge(g_q, t1.n)
                    rope_products(slot[2][:], q_cos, q_sin).then_inc(d_q, 1)
                if t3.exists():
                    dve.wait_ge(t_cs, t3.n + 1)
                    nc.vector.tensor_reduce(cmax[:], by_head(slot[0][:], SEQ), AX_X, ALU.max).then_inc(d_cmax, 1)
                    dve.wait_ge(d_cmax, t3.n + 1)
                    if t3.exists(1):
                        dve.wait_ge(t_cpT, t3.n)
                    tt(cprobs[:], by_head(slot[0][:], SEQ), for_heads(cmax, SEQ), ALU.subtract).then_inc(d_csub, 1)
                if t4.exists():
                    dve.wait_ge(t_ffn, t4.n + 1)
                    if t4.exists(1):
                        dve.wait_ge(g_biased, t4.n)
                    tt(f_scaled[:], bank[1][:, 0:D], fscale[:], ALU.mult).then_inc(d_ffn, 1)
                if t2.exists():
                    dve.wait_ge(a_exp, t2.n + 1)
                    nc.vector.tensor_reduce(psum_[:], probs[:], AX_X, ALU.add).then_inc(d_sum, 1)
                    dve.wait_ge(d_sum, t2.n + 1)
                    nc.vector.reciprocal(pinv[:], psum_[:]).then_inc(d_inv, 1)
                if t1.exists():
                    dve.wait_ge(t_k, t1.n + 1)
                    if t1.exists(1):
                        dve.wait_ge(g_k, t1.n)
                    rope_products(slot[2][:], k_cos, k_sin).then_inc(d_k, 1)
                if t2.exists():
                    dve.wait_ge(t_o, t2.n + 1)
                    dve.wait_ge(d_inv, t2.n + 1)
                    if t2.exists(1):
                        dve.wait_ge(t_oT, t2.n)
                    tt(by_head(o[:], HD), by_head(slot[1][:], HD), for_heads(pinv, HD), ALU.mult).then_inc(d_o, 1)
                if t3.exists():
                    dve.wait_ge(a_cexp, t3.n + 1)
                    nc.vector.tensor_reduce(csum[:], cprobs[:], AX_X, ALU.add).then_inc(d_csum, 1)
                    dve.wait_ge(d_csum, t3.n + 1)
                    nc.vector.reciprocal(cinv[:], csum[:]).then_inc(d_cinv, 1)
                if t4.exists():
                    dve.wait_ge(g_biased, t4.n + 1)
                    if t4.exists(1):
                        dve.wait_ge(g_y, t4.n)
                    nc.vector.tensor_scalar(f_clipped[:], f_biased[:], CLIP, -CLIP, ALU.min,
                                            ALU.max).then_inc(d_clipped, 1)
                if t0.exists():
                    dve.wait_ge(a_xT, t0.n + 1)
                    tt(xnT_lo[:], bank[0][:, 0:P], xnT_hi[:].bitcast(F32), ALU.subtract).then_inc(d_xlo, 1)
                if t3.exists():
                    dve.wait_ge(t_co, t3.n + 1)
                    dve.wait_ge(d_cinv, t3.n + 1)
                    if t3.exists(1):
                        dve.wait_ge(t_coT, t3.n)
                    tt(by_head(co[:], CHD), by_head(bank[1][:, 0:D], CHD), for_heads(cinv, CHD),
                       ALU.mult).then_inc(d_co, 1)
                if t2.exists():
                    dve.wait_ge(t_out, t2.n + 1)
                    dve.wait_ge(g_xres, t2.n + 1)
                    if t2.exists(1):
                        dve.wait_ge(g_x1bo, t2.n)
                    tt(x1[:], bank[1][:, 0:D], x_res[t2.par][:], ALU.add).then_inc(d_x1, 1)
                    dve.wait_ge(d_x1, t2.n + 1)
                    mean_and_variance(t2, 1, x1[:])
                if t3.exists():
                    dve.wait_ge(t_cout, t3.n + 1)
                    dve.wait_ge(g_x1bo, t3.n + 1)
                    if t3.exists(1):
                        dve.wait_ge(g_x2n, t3.n)
                        dve.wait_ge(g_y, t3.n)
                    tt(x2[:], bank[1][:, 0:D], x1_bo[t3.par][:], ALU.add).then_inc(d_x2, 1)
                    dve.wait_ge(d_x2, t3.n + 1)
                    mean_and_variance(t3, 2, x2[:])

            run(dve, step)

        @block.gpsimd
        def _(pool):
            tt = nc.gpsimd.tensor_tensor
            nc.gpsimd.memset(k_bd[:], 0.0)
            for i in range(2):
                nc.gpsimd.memset(v_bd[i][:], 0.0)
            nc.gpsimd.memset(cv_bd[:], 0.0)
            nc.gpsimd.memset(eps[:], EPS)
            nc.gpsimd.memset(zero[:], 0.0)
            nc.gpsimd.memset(neg_half[:], -0.5).then_inc(pool_setup, 1)
            pool.wait_ge(pool_setup, 1)
            pool.wait_ge(weights_in, ALL_WEIGHTS)

            def centre_and_root(t, k, src):
                pool.wait_ge(d_mv[k], t.n + 1)
                tt(veps[k][:], mv[k][:, 1:2], eps[:], ALU.add).then_inc(g_veps[k], 1)
                tt(centred[k][:], src, mv[k][:, 0:1].broadcast_to([P, D]), ALU.subtract)
                pool.wait_ge(g_veps[k], t.n + 1)
                tt(rstd[k][:], veps[k][:], neg_half[:], ALU.pow).then_inc(g_rstd[k], 1)
                pool.wait_ge(g_rstd[k], t.n + 1)

            def rope_sum(dst, with_cos, with_sin):
                d, c, s = (a[:].rearrange("p (h a i) -> p h a i", a=2, i=HD // 2) for a in (dst, with_cos, with_sin))
                tt(d[:, :, 0, :], c[:, :, 0, :], s[:, :, 1, :], ALU.add)
                return tt(d[:, :, 1, :], c[:, :, 1, :], s[:, :, 0, :], ALU.add)

            def scaled(dst, k):
                return tt(dst[:], centred[k][:], rstd[k][:].broadcast_to([P, D]), ALU.mult)

            def step(s):
                t0, t1, t2, t3, t4 = (s.tile(phase) for phase in range(5))
                if t0.exists():
                    centre_and_root(t0, 0, x_in[t0.par][:])
                    if t0.exists(1):
                        pool.wait_ge(t_xT, t0.n)
                    scaled(xn, 0).then_inc(g_xn, 1)
                if t1.exists():
                    pool.wait_ge(d_q, t1.n + 1)
                    if t1.exists(1):
                        pool.wait_ge(t_qT, t1.n)
                    rope_sum(q_rot, q_cos, q_sin).then_inc(g_q, 1)
                if t1.exists():
                    pool.wait_ge(x_loaded[t1.par], t1.landed)
                    if t1.exists(2):
                        pool.wait_ge(d_x1, t1.n - 1)
                    tt(x_res[t1.par][:], x_in[t1.par][:], zero[:].broadcast_to([P, D]), ALU.add).then_inc(g_xres, 1)
                if t4.exists():
                    pool.wait_ge(d_ffn, t4.n + 1)
                    if t4.exists(1):
                        pool.wait_ge(d_clipped, t4.n)
                    tt(f_biased[:], f_scaled[:], fbias[:], ALU.add).then_inc(g_biased, 1)
                if t1.exists():
                    pool.wait_ge(d_k, t1.n + 1)
                    if t1.exists(1):
                        pool.wait_ge(t_kT, t1.n)
                    rope_sum(k_rot, k_cos, k_sin).then_inc(g_k, 1)
                if t4.exists():
                    pool.wait_ge(d_clipped, t4.n + 1)
                    if t4.exists(2):
                        pool.wait_ge(y_stored[t4.par], t4.landed - 16)
                    tt(y[t4.par][:], f_clipped[:], x2[:], ALU.add).then_inc(g_y, 1)
                if t2.exists():
                    centre_and_root(t2, 1, x1[:])
                    if t2.exists(1):
                        pool.wait_ge(t_x1T, t2.n)
                    scaled(x1n, 1).then_inc(g_x1n, 1)
                    if t2.exists(2):
                        pool.wait_ge(d_x2, t2.n - 1)
                    tt(x1_bo[t2.par][:], x1[:], cbo[:], ALU.add).then_inc(g_x1bo, 1)
                if t3.exists():
                    centre_and_root(t3, 2, x2[:])
                    if t3.exists(1):
                        pool.wait_ge(t_x2T, t3.n)
                    scaled(x2n, 2).then_inc(g_x2n, 1)

            run(pool, step)


def _constants():
    pos = np.arange(P) % SEQ
    freqs = (1.0 / 10000.0 ** (np.arange(0, HD, 2, dtype=np.float32) / np.float32(HD))).astype(np.float32)
    angles = (np.arange(SEQ, dtype=np.float32)[:, None] * freqs[None, :]).astype(np.float32)[pos]
    cos, sin = np.cos(angles).astype(np.float32), np.sin(angles).astype(np.float32)
    rope = np.stack([np.concatenate([cos, cos], 1), np.concatenate([sin, -sin], 1)])
    keys = np.arange(BANK) % SEQ
    mask = np.where(keys[None, :] <= pos[:, None], 0.0, MASKED).astype(np.float32)
    head = np.arange(P) // CHD
    groups = np.stack([head[:, None] // GROUP == np.arange(GROUP), head[:, None] % GROUP == np.arange(GROUP)])
    return np.eye(P, dtype=np.float32), mask, rope.astype(np.float32), groups.astype(np.float32)


def kernel(x, ctx_1024, L0_attn_W_qkv, L0_attn_W_out, L0_xattn_Wq, L0_xattn_bq, L0_xattn_Wk, L0_xattn_bk,
           L0_xattn_Wv, L0_xattn_bv, L0_xattn_Wo, L0_xattn_bo, L0_ffn_weights, L0_ffn_scale, L0_ffn_bias):
    import concourse.bacc as _bacc
    from concourse.bass_utils import run_bass_kernel_spmd as _run

    a = np.asarray
    B, S, _ = x.shape
    wqkv = a(L0_attn_W_qkv).reshape(D, 3, H, HD)
    qk = wqkv[:, :2].reshape(D, 2, H, HD // 2, 2).transpose(1, 0, 2, 4, 3).reshape(2, D, F)
    wv = wqkv[:, 2].reshape(D, PAIRS, 2, HD).transpose(0, 2, 1, 3).reshape(D, 2, F // 2)
    wo = a(L0_attn_W_out).reshape(PAIRS, 2 * HD, D).transpose(1, 0, 2)
    cwv = a(L0_xattn_Wv).T.reshape(D, PAIRS, 2, CHD).transpose(0, 2, 1, 3).reshape(D, 2, D // 2)
    cbv = a(L0_xattn_bv).reshape(PAIRS, 2, CHD).transpose(1, 0, 2).reshape(2, D // 2)
    ident, mask, rope, groups = _constants()
    arrays = {
        "x": a(x).reshape(B * S, D), "ctx": a(ctx_1024).reshape(B * S, D), "w_q": qk[0], "w_k": qk[1],
        "w_v": wv, "w_o": wo, "c_wq": a(L0_xattn_Wq).T, "c_wk": a(L0_xattn_Wk).T, "c_wv": cwv,
        "c_wo": a(L0_xattn_Wo).T, "c_bq": a(L0_xattn_bq).reshape(D, 1), "c_bk": a(L0_xattn_bk).reshape(D, 1),
        "c_bv": cbv, "c_bo": a(L0_xattn_bo).reshape(1, D), "f_w": a(L0_ffn_weights).T,
        "f_scale": a(L0_ffn_scale).reshape(1, D), "f_bias": a(L0_ffn_bias).reshape(1, D),
        "ident": ident, "mask": mask, "rope": rope, "groups": groups,
    }
    arrays = {f"in_{k}": np.ascontiguousarray(v) for k, v in arrays.items()}
    nc = _bacc.Bacc("TRN2", target_bir_lowering=False, num_devices=1)
    args = [nc.dram_tensor(k, v.shape, mybir.dt.from_np(v.dtype), kind="ExternalInput").ap()
            for k, v in arrays.items()]
    args.append(nc.dram_tensor("out_y", (B * S, D), F32, kind="ExternalOutput").ap())
    decoder_layer(nc, *args)
    r = _run(nc, [arrays], core_ids=[0])
    return r.results[0]["out_y"].reshape(B, S, D)
```

```python
from contextlib import ExitStack

import numpy as np

import concourse.bass as bass
from concourse import mybir

F32 = mybir.dt.float32
F32R = mybir.dt.float32r
BF16 = mybir.dt.bfloat16
ALU = mybir.AluOpType
ACT = mybir.ActivationFunctionType
AX_X = mybir.AxisListType.X

P = 128
D = 128
SEQ = 64
NB = P // SEQ
H = 16
PAIRS = H // 2
HD = 64
CHD = D // H
F = H * HD
BANK = 512
GROUP = 4
QUAD = GROUP * CHD
EPS = 1e-5
CLIP = 100.0
MASKED = -1e30


def decoder_layer(nc, x, ctx_in, w_q, w_k, w_v, w_o, c_wq, c_wk, c_wv, c_wo, c_bq, c_bk, c_bv,
                  c_bo, f_w, f_scale, f_bias, ident_in, mask_in, rope_in, group_in, out):
    NT = x.shape[0] // P
    LAST_STAGE = 6
    FIRST_STEP, LAST_STEP = -1, NT - 2 + LAST_STAGE
    LOOP_FROM, LOOP_TO = (LAST_STAGE + 2) // 2 * 2, NT - 2

    with ExitStack() as ctx:
        def sb(name, shape, dt=F32):
            return ctx.enter_context(nc.sbuf_tensor(name, shape, dt))

        def sem(name):
            return ctx.enter_context(nc.semaphore(name))

        slot = [ctx.enter_context(nc.psum_tensor(f"slot{i}", [P, 2 * BANK], F32)) for i in range(3)]
        bank = [ctx.enter_context(nc.psum_tensor(f"bank{i}", [P, BANK], F32)) for i in range(2)]

        w_qk = [sb(f"w_qk{i}", [P, F]) for i in range(2)]
        w_qk_hi = [sb(f"w_qk_hi{i}", [P, F], F32R) for i in range(2)]
        w_qk_lo = [sb(f"w_qk_lo{i}", [P, F], F32R) for i in range(2)]
        wv = sb("wv", [P, 2, F // 2])
        wo = sb("wo", [P, PAIRS, D])
        cwq = sb("cwq", [P, D])
        cwk = sb("cwk", [P, D])
        cwv = sb("cwv", [P, 2, D // 2])
        cwo = sb("cwo", [P, D])
        cbq = sb("cbq", [P, 1])
        cbk = sb("cbk", [P, 1])
        cbv = sb("cbv", [P, 1])
        cbo = sb("cbo", [P, D])
        fw_raw = sb("fw_raw", [P, D])
        fw = sb("fw", [P, D])
        fscale = sb("fscale", [P, D])
        fbias = sb("fbias", [P, D])
        ident = sb("ident", [P, P])
        ident_b = sb("ident_b", [P, P], BF16)
        mask_f = sb("mask_f", [P, BANK])
        mask_b = sb("mask_b", [P, BANK], BF16)
        rope_c = sb("rope_c", [P, HD])
        rope_s = sb("rope_s", [P, HD])
        gmask = sb("gmask", [P, GROUP])
        jmask = sb("jmask", [P, GROUP])
        neg_half = sb("neg_half", [P, 1])
        eps = sb("eps", [P, 1])
        zero = sb("zero", [P, 1])
        after_stats = sb("after_stats", [P, 1])

        x_in = [sb(f"x_in{i}", [P, D]) for i in range(2)]
        c_in = [sb(f"c_in{i}", [P, D]) for i in range(2)]
        x_res = [sb(f"x_res{i}", [P, D]) for i in range(2)]
        stats = [sb(f"stats{i}", [P, 6]) for i in range(3)]
        mv = [sb(f"mv{i}", [P, 2]) for i in range(3)]
        veps = [sb(f"veps{i}", [P, 1]) for i in range(3)]
        rstd = [sb(f"rstd{i}", [P, 1]) for i in range(3)]
        centred = [sb(f"centred{i}", [P, D]) for i in range(3)]
        xn = sb("xn", [P, D])
        xnT = sb("xnT", [P, P])
        xnT_hi = sb("xnT_hi", [P, P], F32R)
        xnT_lo = sb("xnT_lo", [P, P], F32R)
        q_cos = sb("q_cos", [P, F])
        q_sin = sb("q_sin", [P, F])
        k_cos = sb("k_cos", [P, F])
        k_sin = sb("k_sin", [P, F])
        q_rot = sb("q_rot", [P, F])
        k_rot = sb("k_rot", [P, F])
        qT = sb("qT", [P, PAIRS, P])
        k_bd = sb("k_bd", [P, PAIRS, NB, 2, SEQ])
        v_bd = [sb(f"v_bd{i}", [P, NB, PAIRS, 2, HD]) for i in range(2)]
        probs = sb("probs", [P, H, SEQ])
        pmax = sb("pmax", [P, H])
        psum_ = sb("psum_", [P, H])
        pinv = sb("pinv", [P, H])
        pT = sb("pT", [P, PAIRS, P])
        o = sb("o", [P, F])
        oT = sb("oT", [P, PAIRS, P])
        x1 = sb("x1", [P, D])
        x1_bo = [sb(f"x1_bo{i}", [P, D]) for i in range(2)]
        x1n = sb("x1n", [P, D])
        x1nT = sb("x1nT", [P, P])
        ctxT = sb("ctxT", [P, P])
        cq_g = sb("cq_g", [P, GROUP, P])
        ck_j = sb("ck_j", [P, GROUP, P])
        cv_bd = sb("cv_bd", [P, NB, PAIRS, QUAD])
        cprobs = sb("cprobs", [P, H, SEQ])
        cmax = sb("cmax", [P, H])
        csum = sb("csum", [P, H])
        cinv = sb("cinv", [P, H])
        cpT = sb("cpT", [P, PAIRS, P])
        coT = sb("coT", [P, P])
        x2 = [sb(f"x2{i}", [P, D]) for i in range(2)]
        x2n = sb("x2n", [P, D])
        x2nT = sb("x2nT", [P, P])
        f_scaled = sb("f_scaled", [P, D])
        f_biased = sb("f_biased", [P, D])
        f_clipped = sb("f_clipped", [P, D])
        y = [sb(f"y{i}", [P, D]) for i in range(2)]

        weights_in = sem("weights_in")
        x_loaded = [sem(f"x_loaded{i}") for i in range(2)]
        ctx_loaded = [sem(f"ctx_loaded{i}") for i in range(2)]
        y_stored = [sem(f"y_stored{i}") for i in range(2)]
        act_setup, dve_setup, pool_setup, fw_doubled = map(sem, ["act_setup", "dve_setup", "pool_setup", "fw_doubled"])
        t_xT, t_q, t_k, t_v, t_qT, t_kT = map(sem, ["t_xT", "t_q", "t_k", "t_v", "t_qT", "t_kT"])
        t_s, t_pT, t_o, t_oT, t_out = map(sem, ["t_s", "t_pT", "t_o", "t_oT", "t_out"])
        t_x1T, t_cq, t_ctxT, t_ck, t_cv = map(sem, ["t_x1T", "t_cq", "t_ctxT", "t_ck", "t_cv"])
        t_cs, t_cpT, t_co, t_cout = map(sem, ["t_cs", "t_cpT", "t_co", "t_cout"])
        t_x2T, t_ffn = map(sem, ["t_x2T", "t_ffn"])
        a_xT, a_v, a_qT, a_k, a_exp = map(sem, ["a_xT", "a_v", "a_qT", "a_k", "a_exp"])
        a_pT, a_oT, a_x1T, a_ctxT, a_cexp = map(sem, ["a_pT", "a_oT", "a_x1T", "a_ctxT", "a_cexp"])
        a_cpT, a_coT, a_x2T, a_cv = map(sem, ["a_cpT", "a_coT", "a_x2T", "a_cv"])
        d_stats = [sem(f"d_stats{i}") for i in range(3)]
        d_mv = [sem(f"d_mv{i}") for i in range(3)]
        d_xlo, d_q, d_k, d_max, d_sub, d_sum, d_inv, d_o, d_x1 = map(
            sem, ["d_xlo", "d_q", "d_k", "d_max", "d_sub", "d_sum", "d_inv", "d_o", "d_x1"])
        d_cq, d_ck, d_cmax, d_csub, d_csum, d_cinv, d_x2 = map(
            sem, ["d_cq", "d_ck", "d_cmax", "d_csub", "d_csum", "d_cinv", "d_x2"])
        d_ffn, d_clipped = map(sem, ["d_ffn", "d_clipped"])
        g_veps = [sem(f"g_veps{i}") for i in range(3)]
        g_rstd = [sem(f"g_rstd{i}") for i in range(3)]
        g_xn, g_x1n, g_x2n, g_xres, g_q, g_k, g_x1bo, g_cprobs, g_biased, g_y = map(
            sem, ["g_xn", "g_x1n", "g_x2n", "g_xres", "g_q", "g_k", "g_x1bo", "g_cprobs", "g_biased", "g_y"])

        class Tile:

            def __init__(self, base, off):
                self.base, self.off = base, off
                self.looped = not isinstance(base, int)
                self.n = base + off
                self.par = (off if self.looped else base + off) % 2
                self.landed = (self.n - self.par) * 8 + 16

            def exists(self, before=0):
                return self.looped or 0 <= self.n - before < NT

        class Step:

            def __init__(self, base, off=0):
                self.base, self.off = base, off

            def tile(self, stage):
                return Tile(self.base, self.off + 1 - stage)

        def run(eng, body):
            for s in range(FIRST_STEP, LOOP_FROM):
                body(Step(s))
            with eng.Fori(LOOP_FROM, LOOP_TO - 1, 2) as s:
                body(Step(s, 0))
                body(Step(s, 1))
            for s in range(LOOP_TO, LAST_STEP + 1):
                body(Step(s))

        Q_T, SCORES, C_PROBS_T, O_T = range(4)
        in_slot0 = [(2, a_qT), (2, d_sub), (5, a_cpT), (3, a_oT)]
        q_t_psum = scores_psum = c_probs_t_psum = o_t_psum = slot[0]
        C_SCORES, K, ATTEND, V = range(4)
        in_slot1 = [(5, d_csub), (1, d_k), (3, d_o), (1, a_v)]
        c_scores_psum = k_psum = attend_psum = v_psum = slot[1]
        K_T, PROBS_T, Q = range(3)
        in_slot2 = [(2, a_k), (3, a_pT), (1, d_q)]
        k_t_psum = probs_t_psum = q_psum = slot[2]
        X_T, C_OUT, X2_T, FFN, C_K = range(5)
        in_bank0 = [(1, d_xlo), (6, d_x2), (6, a_x2T), (6, d_ffn), (4, d_ck)]
        x_psum = c_out_psum = x2_psum = ffn_psum = c_k_psum = bank[0]
        C_ATTEND, OUT, C_V, CTX_T, X1_T, C_Q = range(6)
        in_bank1 = [(6, a_coT), (4, d_x1), (5, a_cv), (4, a_ctxT), (4, a_x1T), (4, d_cq)]
        c_attend_psum = out_psum = c_v_psum = ctx_psum = x1_psum = c_q_psum = bank[1]

        def read_out(held, me, s):
            for back in range(1, (LAST_STAGE + 1) * len(held)):
                stage, read = held[(me - back) % len(held)]
                tile = Tile(s.base, s.off + 1 - stage - (len(held) - 1 - me + back) // len(held))
                if tile.exists():
                    return read, tile.n + 1
            return pool_setup, 1

        load_list = [
            (w_qk[0][:], w_q), (w_qk[1][:], w_k), (wv[:], w_v), (wo[:], w_o), (cwq[:], c_wq), (cwk[:], c_wk),
            (cwv[:], c_wv), (cwo[:], c_wo), (cbq[:], c_bq), (cbk[:], c_bk), (cbv[:], c_bv),
            (cbo[:], c_bo.broadcast_to([P, D])), (fw_raw[:], f_w),
            (fscale[:], f_scale.broadcast_to([P, D])), (fbias[:], f_bias.broadcast_to([P, D])),
            (ident[:], ident_in), (mask_f[:], mask_in), (rope_c[:], rope_in[0]), (rope_s[:], rope_in[1]),
            (gmask[:], group_in[0]), (jmask[:], group_in[1]),
        ]
        ALL_WEIGHTS = 16 * len(load_list)

        def halves(a):
            return [a[:, i * BANK:(i + 1) * BANK] for i in range(F // BANK)]

        def squares(a):
            return [a[:, i * P:(i + 1) * P] for i in range(F // P)]

        def seq(b):
            return slice(b * SEQ, (b + 1) * SEQ)

        def for_heads(a, width):
            return a[:].unsqueeze(2).broadcast_to([P, H, width])

        block = ctx.enter_context(nc.Block())

        @block.sync
        def _(sp):
            def load_x(t):
                if t.exists():
                    if t.exists(2):
                        sp.wait_ge(g_xres, t.n - 1)
                        sp.wait_ge(g_xn, t.n - 1)
                    sp.dma_start(x_in[t.par][:], x[bass.ds(t.n * P, P), :]).then_inc(x_loaded[t.par], 16)

            load_x(Tile(0, 0))
            for dst, src in load_list:
                sp.dma_start(dst, src).then_inc(weights_in, 16)

            def step(s):
                t = s.tile(3)
                if t.exists():
                    if t.exists(2):
                        sp.wait_ge(t_ctxT, t.n - 1)
                    sp.dma_start(c_in[t.par][:], ctx_in[bass.ds(t.n * P, P), :]).then_inc(ctx_loaded[t.par], 16)
                load_x(Tile(s.base, s.off + 2))
                t = s.tile(6)
                if t.exists():
                    sp.wait_ge(g_y, t.n + 1)
                    sp.dma_start(out[bass.ds(t.n * P, P), :], y[t.par][:]).then_inc(y_stored[t.par], 16)

            run(sp, step)
            for t in (Tile(NT - 2, 0), Tile(NT - 1, 0)):
                sp.wait_ge(y_stored[t.par], t.landed)

        @block.tensor
        def _(pe):
            mm, transpose = nc.tensor.matmul, nc.tensor.transpose
            pe.wait_ge(weights_in, ALL_WEIGHTS)
            pe.wait_ge(dve_setup, 1)
            pe.wait_ge(pool_setup, 1)

            def context_v():
                for b in range(NB):
                    for par in range(2):
                        last = mm(c_v_psum[seq(par), b * (D // 2):(b + 1) * (D // 2)], ctxT[:, seq(b)],
                                  cwv[:, par, :], start=True, stop=True, skip_group_check=True)
                return last

            def scores():
                for half, cols in enumerate(halves(scores_psum)):
                    mm(cols, ident_b[:], mask_b[:], start=True, stop=False, skip_group_check=True)
                    for pair in range(half * PAIRS // 2, (half + 1) * PAIRS // 2):
                        for b in range(NB):
                            last = mm(scores_psum[seq(b), pair * P:(pair + 1) * P], qT[:, pair, seq(b)],
                                      k_bd[:, pair, b, :, :].rearrange("p a k -> p (a k)"),
                                      start=False, stop=True, skip_group_check=True)
                return last

            def v_proj():
                for b, cols in enumerate(halves(v_psum)):
                    for par in range(2):
                        last = mm(cols[seq(par), :], xnT[:, seq(b)], wv[:, par, :], start=True, stop=True,
                                  skip_group_check=True)
                return last

            def qk_proj(psum, which):
                hi, lo = halves(w_qk_hi[which]), halves(w_qk_lo[which])
                for cols, w_hi, w_lo in zip(halves(psum), hi, lo):
                    mm(cols, xnT_hi[:], w_hi, start=True, stop=False)
                    mm(cols, xnT_hi[:], w_lo, start=False, stop=False)
                    last = mm(cols, xnT_lo[:], w_hi, start=False, stop=True)
                return last

            def cross_scores():
                width = GROUP * SEQ
                for g in range(GROUP):
                    for b in range(NB):
                        last = mm(c_scores_psum[seq(b), g * width:(g + 1) * width], cq_g[:, g, seq(b)],
                                  ck_j[:, :, seq(b)], start=True, stop=True, skip_group_check=True)
                return last

            def attend(t):
                for pair in range(PAIRS):
                    for b in range(NB):
                        last = mm(attend_psum[seq(b), pair * P:(pair + 1) * P], pT[:, pair, seq(b)],
                                  v_bd[t.par][:, b, pair, :, :].rearrange("p a k -> p (a k)"),
                                  start=True, stop=True, skip_group_check=True)
                return last

            def cross_attend():
                for b in range(NB):
                    for k in range(2):
                        for g in range(GROUP):
                            pair = 2 * g + k
                            last = mm(c_attend_psum[g * QUAD:(g + 1) * QUAD, seq(b)], cv_bd[:, b, pair, :],
                                      cpT[:, pair, seq(b)], start=k == 0, stop=k == 1, skip_group_check=True)
                return last

            def out_proj():
                for pair in range(PAIRS):
                    last = mm(out_psum[:, 0:D], oT[:, pair, :], wo[:, pair, :],
                              start=pair == 0, stop=pair == PAIRS - 1)
                return last

            def transposes(psum, src):
                for to, squares_of in zip(squares(psum), squares(src)):
                    last = transpose(to, squares_of, ident[:])
                return last

            def step(s):
                t0, t1, t2, t3, t4, t5, t6 = (s.tile(stage) for stage in range(7))
                if t6.exists():
                    pe.wait_ge(*read_out(in_bank1, C_ATTEND, s))
                    pe.wait_ge(a_cv, t6.n + 1)
                    pe.wait_ge(a_cpT, t6.n + 1)
                    cross_attend().then_inc(t_co, 1)
                if t1.exists():
                    pe.wait_ge(*read_out(in_bank0, X_T, s))
                    pe.wait_ge(g_xn, t1.n + 1)
                    transpose(x_psum[:, 0:P], xn[:], ident[:]).then_inc(t_xT, 1)
                if t5.exists():
                    pe.wait_ge(*read_out(in_slot1, C_SCORES, s))
                    pe.wait_ge(d_ck, t5.n + 1)
                    pe.wait_ge(d_cq, t5.n + 1)
                    cross_scores().then_inc(t_cs, 1)
                if t2.exists():
                    pe.wait_ge(*read_out(in_slot2, K_T, s))
                    pe.wait_ge(g_k, t2.n + 1)
                    transposes(k_t_psum, k_rot[:]).then_inc(t_kT, 1)
                if t6.exists():
                    pe.wait_ge(*read_out(in_bank0, C_OUT, s))
                    pe.wait_ge(a_coT, t6.n + 1)
                    mm(c_out_psum[:, 0:D], coT[:], cwo[:], start=True, stop=True).then_inc(t_cout, 1)
                if t4.exists():
                    pe.wait_ge(*read_out(in_bank1, OUT, s))
                    pe.wait_ge(a_oT, t4.n + 1)
                    out_proj().then_inc(t_out, 1)
                if t2.exists():
                    pe.wait_ge(*read_out(in_slot0, Q_T, s))
                    pe.wait_ge(g_q, t2.n + 1)
                    transposes(q_t_psum, q_rot[:]).then_inc(t_qT, 1)
                if t1.exists():
                    pe.wait_ge(*read_out(in_slot1, K, s))
                    pe.wait_ge(d_xlo, t1.n + 1)
                    qk_proj(k_psum, 1).then_inc(t_k, 1)
                if t3.exists():
                    pe.wait_ge(*read_out(in_slot2, PROBS_T, s))
                    pe.wait_ge(a_exp, t3.n + 1)
                    transposes(probs_t_psum, probs[:].rearrange("p h k -> p (h k)")).then_inc(t_pT, 1)
                if t5.exists():
                    pe.wait_ge(*read_out(in_bank1, C_V, s))
                    pe.wait_ge(a_ctxT, t5.n + 1)
                    context_v().then_inc(t_cv, 1)
                if t6.exists():
                    pe.wait_ge(*read_out(in_bank0, X2_T, s))
                    pe.wait_ge(g_x2n, t6.n + 1)
                    transpose(x2_psum[:, 0:P], x2n[:], ident[:]).then_inc(t_x2T, 1)
                if t2.exists():
                    pe.wait_ge(*read_out(in_slot0, SCORES, s))
                    pe.wait_ge(a_qT, t2.n + 1)
                    pe.wait_ge(a_k, t2.n + 1)
                    scores().then_inc(t_s, 1)
                if t4.exists():
                    pe.wait_ge(*read_out(in_bank1, CTX_T, s))
                    pe.wait_ge(ctx_loaded[t4.par], t4.landed)
                    transpose(ctx_psum[:, 0:P], c_in[t4.par][:], ident[:]).then_inc(t_ctxT, 1)
                if t6.exists():
                    pe.wait_ge(*read_out(in_bank0, FFN, s))
                    pe.wait_ge(a_x2T, t6.n + 1)
                    mm(ffn_psum[:, 0:D], x2nT[:], fw[:], start=True, stop=True).then_inc(t_ffn, 1)
                if t3.exists():
                    pe.wait_ge(*read_out(in_slot1, ATTEND, s))
                    pe.wait_ge(a_v, t3.n + 1)
                    pe.wait_ge(a_pT, t3.n + 1)
                    attend(t3).then_inc(t_o, 1)
                if t4.exists():
                    pe.wait_ge(*read_out(in_bank1, X1_T, s))
                    pe.wait_ge(g_x1n, t4.n + 1)
                    transpose(x1_psum[:, 0:P], x1n[:], ident[:]).then_inc(t_x1T, 1)
                if t1.exists():
                    pe.wait_ge(*read_out(in_slot2, Q, s))
                    pe.wait_ge(d_xlo, t1.n + 1)
                    qk_proj(q_psum, 0).then_inc(t_q, 1)
                if t4.exists():
                    pe.wait_ge(*read_out(in_bank0, C_K, s))
                    pe.wait_ge(a_ctxT, t4.n + 1)
                    mm(c_k_psum[:, 0:P], cwk[:], ctxT[:], start=True, stop=True).then_inc(t_ck, 1)
                if t5.exists():
                    pe.wait_ge(*read_out(in_slot0, C_PROBS_T, s))
                    pe.wait_ge(g_cprobs, t5.n + 1)
                    transposes(c_probs_t_psum, cprobs[:].rearrange("p h k -> p (h k)")).then_inc(t_cpT, 1)
                if t4.exists():
                    pe.wait_ge(*read_out(in_bank1, C_Q, s))
                    pe.wait_ge(a_x1T, t4.n + 1)
                    mm(c_q_psum[:, 0:P], cwq[:], x1nT[:], start=True, stop=True).then_inc(t_cq, 1)
                if t1.exists():
                    pe.wait_ge(*read_out(in_slot1, V, s))
                    pe.wait_ge(a_xT, t1.n + 1)
                    v_proj().then_inc(t_v, 1)
                if t3.exists():
                    pe.wait_ge(*read_out(in_slot0, O_T, s))
                    pe.wait_ge(d_o, t3.n + 1)
                    transposes(o_t_psum, o[:]).then_inc(t_oT, 1)

            run(pe, step)

        @block.scalar
        def _(act):
            copy = nc.scalar.copy
            act.wait_ge(weights_in, ALL_WEIGHTS)
            for i in range(2):
                last = copy(w_qk_hi[i][:], w_qk[i][:])
            last.then_inc(act_setup, 1)
            act.wait_ge(pool_setup, 1)

            def wide(a):
                return a[:].rearrange("p r t -> p (r t)")

            def diagonal(blocks, par):
                first = blocks[seq(par), 0, 0, par * CHD:(par + 1) * CHD]
                return bass.AP(first.tensor, first.offset,
                               [first.ap[0], [2 * QUAD, NB * GROUP], [QUAD + 2 * CHD, 2], [1, CHD]])

            def step(s):
                t0, t1, t2, t3, t4, t5, t6 = (s.tile(stage) for stage in range(7))
                if t6.exists():
                    act.wait_ge(t_co, t6.n + 1)
                    if t6.exists(1):
                        act.wait_ge(t_cout, t6.n)
                    nc.scalar.activation(coT[:], c_attend_psum[:, 0:P], ACT.Identity, bias=cbv[:]).then_inc(a_coT, 1)
                if t1.exists():
                    act.wait_ge(t_xT, t1.n + 1)
                    if t1.exists(1):
                        act.wait_ge(t_v, t1.n)
                    copy(xnT[:], x_psum[:, 0:P])
                    copy(xnT_hi[:], x_psum[:, 0:P]).then_inc(a_xT, 1)
                if t4.exists():
                    act.wait_ge(t_oT, t4.n + 1)
                    if t4.exists(1):
                        act.wait_ge(t_out, t4.n)
                    copy(wide(oT), o_t_psum[:]).then_inc(a_oT, 1)
                if t2.exists():
                    act.wait_ge(t_kT, t2.n + 1)
                    if t2.exists(1):
                        act.wait_ge(t_s, t2.n)
                    for par in range(2):
                        last = copy(k_bd[seq(par), :, :, par, :].rearrange("p r b k -> p (r b) k"),
                                    k_t_psum[seq(par), :].rearrange("p (r k) -> p r k", k=SEQ))
                    last.then_inc(a_k, 1)
                if t5.exists():
                    act.wait_ge(d_csub, t5.n + 1)
                    nc.scalar.activation(cprobs[:], cprobs[:], ACT.Exp, scale=float(CHD) ** -0.5).then_inc(a_cexp, 1)
                if t2.exists():
                    act.wait_ge(t_qT, t2.n + 1)
                    if t2.exists(1):
                        act.wait_ge(t_s, t2.n)
                    copy(wide(qT), q_t_psum[:]).then_inc(a_qT, 1)
                if t5.exists():
                    act.wait_ge(t_cv, t5.n + 1)
                    if t5.exists(1):
                        act.wait_ge(t_co, t5.n)
                    for par in range(2):
                        last = copy(diagonal(cv_bd, par), c_v_psum[seq(par), 0:D].rearrange("p (q k d) -> p q k d", k=2, d=CHD))
                    last.then_inc(a_cv, 1)
                if t3.exists():
                    act.wait_ge(t_pT, t3.n + 1)
                    if t3.exists(1):
                        act.wait_ge(t_o, t3.n)
                    copy(wide(pT), probs_t_psum[:]).then_inc(a_pT, 1)
                if t6.exists():
                    act.wait_ge(t_x2T, t6.n + 1)
                    if t6.exists(1):
                        act.wait_ge(t_ffn, t6.n)
                    copy(x2nT[:], x2_psum[:, 0:P]).then_inc(a_x2T, 1)
                if t4.exists():
                    act.wait_ge(t_ctxT, t4.n + 1)
                    if t4.exists(1):
                        act.wait_ge(t_cv, t4.n)
                    copy(ctxT[:], ctx_psum[:, 0:P]).then_inc(a_ctxT, 1)
                if t4.exists():
                    act.wait_ge(t_x1T, t4.n + 1)
                    if t4.exists(1):
                        act.wait_ge(t_cq, t4.n)
                    copy(x1nT[:], x1_psum[:, 0:P]).then_inc(a_x1T, 1)
                if t2.exists():
                    act.wait_ge(d_sub, t2.n + 1)
                    nc.scalar.activation(probs[:], probs[:], ACT.Exp, scale=float(HD) ** -0.5).then_inc(a_exp, 1)
                if t5.exists():
                    act.wait_ge(t_cpT, t5.n + 1)
                    if t5.exists(1):
                        act.wait_ge(t_co, t5.n)
                    copy(wide(cpT), c_probs_t_psum[:]).then_inc(a_cpT, 1)
                if t1.exists():
                    act.wait_ge(t_v, t1.n + 1)
                    if t1.exists(2):
                        act.wait_ge(t_o, t1.n - 1)
                    for par in range(2):
                        last = copy(v_bd[t1.par][seq(par), :, :, par, :].rearrange("p b r d -> p (b r) d"),
                                    v_psum[seq(par), :].rearrange("p (r d) -> p r d", d=HD))
                    last.then_inc(a_v, 1)

            run(act, step)

        @block.vector
        def _(dve):
            tt = nc.vector.tensor_tensor
            dve.wait_ge(weights_in, ALL_WEIGHTS)
            dve.wait_ge(pool_setup, 1)
            nc.vector.tensor_copy(ident_b[:], ident[:])
            nc.vector.tensor_copy(mask_b[:], mask_f[:])
            nc.vector.tensor_scalar(fw[:], fw_raw[:], 0.0, 2.0, ALU.is_ge, ALU.mult).then_inc(fw_doubled, 1)
            dve.wait_ge(fw_doubled, 1)
            nc.vector.tensor_scalar(fw[:], fw[:], 1.0, None, ALU.subtract)
            dve.wait_ge(act_setup, 1)
            for i in range(2):
                last = tt(w_qk_lo[i][:], w_qk[i][:], w_qk_hi[i][:].bitcast(F32), ALU.subtract)
            last.then_inc(dve_setup, 1)

            def mean_and_variance(t, k, src):
                nc.vector.bn_stats(stats[k][:], src).then_inc(d_stats[k], 1)
                dve.wait_ge(d_stats[k], t.n + 1)
                tt(after_stats[:], eps[:], eps[:], ALU.add)
                nc.vector.bn_aggr(mv[k][:], stats[k][:]).then_inc(d_mv[k], 1)

            def by_head(a, width):
                return a.rearrange("p (h d) -> p h d", d=width)

            def rope_products(q_or_k, with_cos, with_sin):
                v = by_head(q_or_k, HD)
                tt(by_head(with_cos[:], HD), v, rope_c[:].unsqueeze(1).broadcast_to([P, H, HD]), ALU.mult)
                return tt(by_head(with_sin[:], HD), v, rope_s[:].unsqueeze(1).broadcast_to([P, H, HD]), ALU.mult)

            def masked_rows(dst, src, bias, masks):
                return nc.vector.scalar_tensor_tensor(
                    out=dst[:], in0=src.unsqueeze(1).broadcast_to([P, GROUP, P]), scalar=bias[:],
                    in1=masks[:].unsqueeze(2).broadcast_to([P, GROUP, P]), op0=ALU.add, op1=ALU.mult)

            def step(s):
                t0, t1, t2, t3, t4, t5, t6 = (s.tile(stage) for stage in range(7))
                if t3.exists():
                    dve.wait_ge(a_exp, t3.n + 1)
                    nc.vector.tensor_reduce(psum_[:], probs[:], AX_X, ALU.add).then_inc(d_sum, 1)
                    dve.wait_ge(d_sum, t3.n + 1)
                    nc.vector.reciprocal(pinv[:], psum_[:]).then_inc(d_inv, 1)
                if t1.exists():
                    dve.wait_ge(a_xT, t1.n + 1)
                    if t1.exists(1):
                        dve.wait_ge(t_q, t1.n)
                    tt(xnT_lo[:], x_psum[:, 0:P], xnT_hi[:].bitcast(F32), ALU.subtract).then_inc(d_xlo, 1)
                if t5.exists():
                    dve.wait_ge(t_cs, t5.n + 1)
                    nc.vector.tensor_reduce(cmax[:], by_head(c_scores_psum[:], SEQ), AX_X, ALU.max).then_inc(d_cmax, 1)
                    dve.wait_ge(d_cmax, t5.n + 1)
                    if t5.exists(1):
                        dve.wait_ge(t_cpT, t5.n)
                    tt(cprobs[:], by_head(c_scores_psum[:], SEQ), for_heads(cmax, SEQ), ALU.subtract).then_inc(d_csub, 1)
                if t6.exists():
                    dve.wait_ge(t_cout, t6.n + 1)
                    dve.wait_ge(g_x1bo, t6.n + 1)
                    if t6.exists(1):
                        dve.wait_ge(g_x2n, t6.n)
                    if t6.exists(2):
                        dve.wait_ge(g_y, t6.n - 1)
                    tt(x2[t6.par][:], c_out_psum[:, 0:D], x1_bo[t6.par][:], ALU.add).then_inc(d_x2, 1)
                    dve.wait_ge(d_x2, t6.n + 1)
                    mean_and_variance(t6, 2, x2[t6.par][:])
                if t4.exists():
                    dve.wait_ge(t_out, t4.n + 1)
                    dve.wait_ge(g_xres, t4.n + 1)
                    if t4.exists(1):
                        dve.wait_ge(g_x1bo, t4.n)
                    tt(x1[:], out_psum[:, 0:D], x_res[t4.par][:], ALU.add).then_inc(d_x1, 1)
                    dve.wait_ge(d_x1, t4.n + 1)
                    mean_and_variance(t4, 1, x1[:])
                if t1.exists():
                    dve.wait_ge(t_k, t1.n + 1)
                    if t1.exists(1):
                        dve.wait_ge(g_k, t1.n)
                    rope_products(k_psum[:], k_cos, k_sin).then_inc(d_k, 1)
                if t5.exists():
                    dve.wait_ge(a_cexp, t5.n + 1)
                    if t5.exists(1):
                        dve.wait_ge(g_cprobs, t5.n)
                    nc.vector.tensor_reduce(csum[:], cprobs[:], AX_X, ALU.add).then_inc(d_csum, 1)
                    dve.wait_ge(d_csum, t5.n + 1)
                    nc.vector.reciprocal(cinv[:], csum[:]).then_inc(d_cinv, 1)
                if t2.exists():
                    dve.wait_ge(t_s, t2.n + 1)
                    nc.vector.tensor_reduce(pmax[:], by_head(scores_psum[:], SEQ), AX_X, ALU.max).then_inc(d_max, 1)
                    dve.wait_ge(d_max, t2.n + 1)
                    if t2.exists(1):
                        dve.wait_ge(t_pT, t2.n)
                    tt(probs[:], by_head(scores_psum[:], SEQ), for_heads(pmax, SEQ), ALU.subtract).then_inc(d_sub, 1)
                if t6.exists():
                    dve.wait_ge(t_ffn, t6.n + 1)
                    if t6.exists(1):
                        dve.wait_ge(g_biased, t6.n)
                    tt(f_scaled[:], ffn_psum[:, 0:D], fscale[:], ALU.mult).then_inc(d_ffn, 1)
                if t3.exists():
                    dve.wait_ge(t_o, t3.n + 1)
                    dve.wait_ge(d_inv, t3.n + 1)
                    if t3.exists(1):
                        dve.wait_ge(t_oT, t3.n)
                    tt(by_head(o[:], HD), by_head(attend_psum[:], HD), for_heads(pinv, HD), ALU.mult).then_inc(d_o, 1)
                if t6.exists():
                    dve.wait_ge(g_biased, t6.n + 1)
                    if t6.exists(1):
                        dve.wait_ge(g_y, t6.n)
                    nc.vector.tensor_scalar(f_clipped[:], f_biased[:], CLIP, -CLIP, ALU.min, ALU.max).then_inc(d_clipped, 1)
                if t4.exists():
                    dve.wait_ge(t_ck, t4.n + 1)
                    if t4.exists(1):
                        dve.wait_ge(t_cs, t4.n)
                    masked_rows(ck_j, c_k_psum[:, 0:P], cbk, jmask).then_inc(d_ck, 1)
                if t4.exists():
                    dve.wait_ge(t_cq, t4.n + 1)
                    if t4.exists(1):
                        dve.wait_ge(t_cs, t4.n)
                    masked_rows(cq_g, c_q_psum[:, 0:P], cbq, gmask).then_inc(d_cq, 1)
                if t0.exists():
                    dve.wait_ge(x_loaded[t0.par], t0.landed)
                    if t0.exists(1):
                        dve.wait_ge(g_xn, t0.n)
                    mean_and_variance(t0, 0, x_in[t0.par][:])
                if t1.exists():
                    dve.wait_ge(t_q, t1.n + 1)
                    if t1.exists(1):
                        dve.wait_ge(g_q, t1.n)
                    rope_products(q_psum[:], q_cos, q_sin).then_inc(d_q, 1)

            run(dve, step)

        @block.gpsimd
        def _(pool):
            tt = nc.gpsimd.tensor_tensor
            nc.gpsimd.memset(k_bd[:], 0.0)
            for i in range(2):
                nc.gpsimd.memset(v_bd[i][:], 0.0)
            nc.gpsimd.memset(cv_bd[:], 0.0)
            nc.gpsimd.memset(eps[:], EPS)
            nc.gpsimd.memset(zero[:], 0.0)
            nc.gpsimd.memset(neg_half[:], -0.5).then_inc(pool_setup, 1)
            pool.wait_ge(pool_setup, 1)
            pool.wait_ge(weights_in, ALL_WEIGHTS)

            def centre_and_root(t, k, src):
                pool.wait_ge(d_mv[k], t.n + 1)
                tt(veps[k][:], mv[k][:, 1:2], eps[:], ALU.add).then_inc(g_veps[k], 1)
                tt(centred[k][:], src, mv[k][:, 0:1].broadcast_to([P, D]), ALU.subtract)
                pool.wait_ge(g_veps[k], t.n + 1)
                tt(rstd[k][:], veps[k][:], neg_half[:], ALU.pow).then_inc(g_rstd[k], 1)
                pool.wait_ge(g_rstd[k], t.n + 1)

            def rope_sum(dst, with_cos, with_sin):
                d, c, s = (a[:].rearrange("p (h a i) -> p h a i", a=2, i=HD // 2) for a in (dst, with_cos, with_sin))
                tt(d[:, :, 0, :], c[:, :, 0, :], s[:, :, 1, :], ALU.add)
                return tt(d[:, :, 1, :], c[:, :, 1, :], s[:, :, 0, :], ALU.add)

            def scaled(dst, k):
                return tt(dst[:], centred[k][:], rstd[k][:].broadcast_to([P, D]), ALU.mult)

            def step(s):
                t0, t1, t2, t3, t4, t5, t6 = (s.tile(stage) for stage in range(7))
                if t2.exists():
                    pool.wait_ge(d_q, t2.n + 1)
                    if t2.exists(1):
                        pool.wait_ge(t_qT, t2.n)
                    rope_sum(q_rot, q_cos, q_sin).then_inc(g_q, 1)
                if t6.exists():
                    centre_and_root(t6, 2, x2[t6.par][:])
                    if t6.exists(1):
                        pool.wait_ge(t_x2T, t6.n)
                    scaled(x2n, 2).then_inc(g_x2n, 1)
                if t4.exists():
                    centre_and_root(t4, 1, x1[:])
                    if t4.exists(1):
                        pool.wait_ge(t_x1T, t4.n)
                    scaled(x1n, 1).then_inc(g_x1n, 1)
                    if t4.exists(2):
                        pool.wait_ge(d_x2, t4.n - 1)
                    tt(x1_bo[t4.par][:], x1[:], cbo[:], ALU.add).then_inc(g_x1bo, 1)
                if t2.exists():
                    pool.wait_ge(x_loaded[t2.par], t2.landed)
                    if t2.exists(2):
                        pool.wait_ge(d_x1, t2.n - 1)
                    tt(x_res[t2.par][:], x_in[t2.par][:], zero[:].broadcast_to([P, D]), ALU.add).then_inc(g_xres, 1)
                if t1.exists():
                    pool.wait_ge(d_k, t1.n + 1)
                    if t1.exists(1):
                        pool.wait_ge(t_kT, t1.n)
                    rope_sum(k_rot, k_cos, k_sin).then_inc(g_k, 1)
                if t5.exists():
                    pool.wait_ge(d_cinv, t5.n + 1)
                    tt(cprobs[:], cprobs[:], for_heads(cinv, SEQ), ALU.mult).then_inc(g_cprobs, 1)
                if t6.exists():
                    pool.wait_ge(d_ffn, t6.n + 1)
                    if t6.exists(1):
                        pool.wait_ge(d_clipped, t6.n)
                    tt(f_biased[:], f_scaled[:], fbias[:], ALU.add).then_inc(g_biased, 1)
                if t6.exists():
                    pool.wait_ge(d_clipped, t6.n + 1)
                    if t6.exists(2):
                        pool.wait_ge(y_stored[t6.par], t6.landed - 16)
                    tt(y[t6.par][:], f_clipped[:], x2[t6.par][:], ALU.add).then_inc(g_y, 1)
                if t0.exists():
                    centre_and_root(t0, 0, x_in[t0.par][:])
                    if t0.exists(1):
                        pool.wait_ge(t_xT, t0.n)
                    scaled(xn, 0).then_inc(g_xn, 1)

            run(pool, step)


def _constants():
    pos = np.arange(P) % SEQ
    freqs = (1.0 / 10000.0 ** (np.arange(0, HD, 2, dtype=np.float32) / np.float32(HD))).astype(np.float32)
    angles = (np.arange(SEQ, dtype=np.float32)[:, None] * freqs[None, :]).astype(np.float32)[pos]
    cos, sin = np.cos(angles).astype(np.float32), np.sin(angles).astype(np.float32)
    rope = np.stack([np.concatenate([cos, cos], 1), np.concatenate([sin, -sin], 1)])
    keys = np.arange(BANK) % SEQ
    mask = np.where(keys[None, :] <= pos[:, None], 0.0, MASKED).astype(np.float32)
    head = np.arange(P) // CHD
    groups = np.stack([head[:, None] // GROUP == np.arange(GROUP), head[:, None] % GROUP == np.arange(GROUP)])
    return np.eye(P, dtype=np.float32), mask, rope.astype(np.float32), groups.astype(np.float32)


def kernel(x, ctx_1024, L0_attn_W_qkv, L0_attn_W_out, L0_xattn_Wq, L0_xattn_bq, L0_xattn_Wk, L0_xattn_bk,
           L0_xattn_Wv, L0_xattn_bv, L0_xattn_Wo, L0_xattn_bo, L0_ffn_weights, L0_ffn_scale, L0_ffn_bias):
    import concourse.bacc as _bacc
    from concourse.bass_utils import run_bass_kernel_spmd as _run

    a = np.asarray
    B, S, _ = x.shape
    wqkv = a(L0_attn_W_qkv).reshape(D, 3, H, HD)
    qk = wqkv[:, :2].reshape(D, 2, H, HD // 2, 2).transpose(1, 0, 2, 4, 3).reshape(2, D, F)
    wv = wqkv[:, 2].reshape(D, PAIRS, 2, HD).transpose(0, 2, 1, 3).reshape(D, 2, F // 2)
    wo = a(L0_attn_W_out).reshape(PAIRS, 2 * HD, D).transpose(1, 0, 2)
    cwv = a(L0_xattn_Wv).T.reshape(D, PAIRS, 2, CHD).transpose(0, 2, 1, 3).reshape(D, 2, D // 2)
    ident, mask, rope, groups = _constants()
    arrays = {
        "x": a(x).reshape(B * S, D), "ctx": a(ctx_1024).reshape(B * S, D), "w_q": qk[0], "w_k": qk[1],
        "w_v": wv, "w_o": wo, "c_wq": a(L0_xattn_Wq).T, "c_wk": a(L0_xattn_Wk).T, "c_wv": cwv,
        "c_wo": a(L0_xattn_Wo).T, "c_bq": a(L0_xattn_bq).reshape(D, 1), "c_bk": a(L0_xattn_bk).reshape(D, 1),
        "c_bv": a(L0_xattn_bv).reshape(D, 1), "c_bo": a(L0_xattn_bo).reshape(1, D), "f_w": a(L0_ffn_weights).T,
        "f_scale": a(L0_ffn_scale).reshape(1, D), "f_bias": a(L0_ffn_bias).reshape(1, D),
        "ident": ident, "mask": mask, "rope": rope, "groups": groups,
    }
    arrays = {f"in_{k}": np.ascontiguousarray(v) for k, v in arrays.items()}
    nc = _bacc.Bacc("TRN2", target_bir_lowering=False, num_devices=1)
    args = [nc.dram_tensor(k, v.shape, mybir.dt.from_np(v.dtype), kind="ExternalInput").ap()
            for k, v in arrays.items()]
    args.append(nc.dram_tensor("out_y", (B * S, D), F32, kind="ExternalOutput").ap())
    decoder_layer(nc, *args)
    r = _run(nc, [arrays], core_ids=[0])
    return r.results[0]["out_y"].reshape(B, S, D)
```

```python
from contextlib import ExitStack

import numpy as np

import concourse.bass as bass
from concourse import mybir

F32 = mybir.dt.float32
F32R = mybir.dt.float32r
ALU = mybir.AluOpType
ACT = mybir.ActivationFunctionType
AX_X = mybir.AxisListType.X

P = 128
D = 128
SEQ = 64
NB = P // SEQ
H = 16
PAIRS = H // 2
HD = 64
CHD = D // H
F = H * HD
BANK = 512
GROUP = 4
QUAD = GROUP * CHD
EPS = 1e-5
CLIP = 100.0
MASKED = -1e30


def decoder_layer(nc, x, ctx_t, w_q, w_k, w_v, w_o, c_wq, c_wk, c_wv, c_wo, c_bq, c_bk, c_bv,
                  c_bo, f_w, f_scale, f_bias, ident_in, mask_in, rope_in, group_in, out):
    NT = x.shape[0] // P
    LAST_STAGE = 6
    LAST_STEP = NT - 2 + LAST_STAGE
    LOOP_FROM, LOOP_TO = (LAST_STAGE + 2) // 2 * 2, NT - 2

    with ExitStack() as ctx:
        def sb(name, shape, dt=F32):
            return ctx.enter_context(nc.sbuf_tensor(name, shape, dt))

        def sem(name):
            return ctx.enter_context(nc.semaphore(name))

        slot = [ctx.enter_context(nc.psum_tensor(f"slot{i}", [P, 2 * BANK], F32)) for i in range(3)]
        bank = [ctx.enter_context(nc.psum_tensor(f"bank{i}", [P, BANK], F32)) for i in range(2)]

        w_qkv = [sb(f"w_qkv{i}", [P, F]) for i in range(3)]
        w_hi = [sb(f"w_hi{i}", [P, F], F32R) for i in range(3)]
        w_lo = [sb(f"w_lo{i}", [P, F], F32R) for i in range(3)]
        wo = sb("wo", [P, PAIRS, D])
        cwq = sb("cwq", [P, D])
        cwk = sb("cwk", [P, D])
        cwv = sb("cwv", [P, 2, D // 2])
        cwo = sb("cwo", [P, D])
        cbq = sb("cbq", [P, 1])
        cbk = sb("cbk", [P, 1])
        cbv = sb("cbv", [P, 1])
        cbo = sb("cbo", [P, D])
        fw_raw = sb("fw_raw", [P, D])
        fw = sb("fw", [P, D])
        fscale = sb("fscale", [P, D])
        fbias = sb("fbias", [P, D])
        ident = sb("ident", [P, P])
        mask = sb("mask", [P, SEQ])
        rope_c = sb("rope_c", [P, HD])
        rope_s = sb("rope_s", [P, HD])
        jmask = sb("jmask", [P, GROUP])
        cbk_j = sb("cbk_j", [P, GROUP])
        neg_half = sb("neg_half", [P, 1])
        eps = sb("eps", [P, 1])
        zero = sb("zero", [P, 1])
        after_stats = sb("after_stats", [P, 1])

        x_in = [sb(f"x_in{i}", [P, D]) for i in range(2)]
        x_res = [sb(f"x_res{i}", [P, D]) for i in range(2)]
        stats = [sb(f"stats{i}", [P, 6]) for i in range(3)]
        mv = [sb(f"mv{i}", [P, 2]) for i in range(3)]
        veps = [sb(f"veps{i}", [P, 1]) for i in range(3)]
        rstd = [sb(f"rstd{i}", [P, 1]) for i in range(3)]
        centred = [sb(f"centred{i}", [P, D]) for i in range(3)]
        xn = sb("xn", [P, D])
        xnT_hi = sb("xnT_hi", [P, P], F32R)
        xnT_lo = sb("xnT_lo", [P, P], F32R)
        q_cos = sb("q_cos", [P, F])
        q_sin = sb("q_sin", [P, F])
        k_cos = sb("k_cos", [P, F])
        k_sin = sb("k_sin", [P, F])
        q_rot = sb("q_rot", [P, F])
        k_rot = sb("k_rot", [P, F])
        qT = sb("qT", [P, PAIRS, P])
        k_bd = sb("k_bd", [P, PAIRS, NB, 2, SEQ])
        v = [sb(f"v{i}", [P, F]) for i in range(2)]
        probs = sb("probs", [P, H, SEQ])
        pmax = sb("pmax", [P, H])
        psum_ = sb("psum_", [P, H])
        pinv = sb("pinv", [P, H])
        p_bd = sb("p_bd", [P, PAIRS, 2, NB, SEQ])
        oT = sb("oT", [P, PAIRS, P])
        x1 = sb("x1", [P, D])
        x1_bo = [sb(f"x1_bo{i}", [P, D]) for i in range(2)]
        x1n = sb("x1n", [P, D])
        x1nT = sb("x1nT", [P, P])
        ctxT = [sb(f"ctxT{i}", [P, P]) for i in range(2)]
        cq_g = sb("cq_g", [P, GROUP, P])
        ck_j = sb("ck_j", [P, GROUP, P])
        cv_bd = sb("cv_bd", [P, NB, PAIRS, QUAD])
        cprobs = sb("cprobs", [P, H, SEQ])
        cmax = sb("cmax", [P, H])
        csum = sb("csum", [P, H])
        cinv = sb("cinv", [P, H])
        cpT = sb("cpT", [P, PAIRS, P])
        coT = sb("coT", [P, P])
        x2 = [sb(f"x2{i}", [P, D]) for i in range(2)]
        x2n = sb("x2n", [P, D])
        x2nT = sb("x2nT", [P, P])
        f_scaled = sb("f_scaled", [P, D])
        f_biased = sb("f_biased", [P, D])
        f_clipped = sb("f_clipped", [P, D])
        y = [sb(f"y{i}", [P, D]) for i in range(2)]

        w_in = [sem(f"w_in{i}") for i in range(3)]
        ident_loaded, rope_loaded, rest_in = map(sem, ["ident_loaded", "rope_loaded", "rest_in"])
        x_loaded = [sem(f"x_loaded{i}") for i in range(2)]
        ctx_loaded = [sem(f"ctx_loaded{i}") for i in range(2)]
        y_stored = [sem(f"y_stored{i}") for i in range(2)]
        act_setup, dve_setup, pool_setup, fw_doubled = map(sem, ["act_setup", "dve_setup", "pool_setup", "fw_doubled"])
        t_xT, t_q, t_k, t_v, t_qT, t_kT = map(sem, ["t_xT", "t_q", "t_k", "t_v", "t_qT", "t_kT"])
        t_s, t_pT, t_o, t_out = map(sem, ["t_s", "t_pT", "t_o", "t_out"])
        t_x1T, t_cq, t_ck, t_cv = map(sem, ["t_x1T", "t_cq", "t_ck", "t_cv"])
        t_cs, t_cpT, t_co, t_cout = map(sem, ["t_cs", "t_cpT", "t_co", "t_cout"])
        t_x2T, t_ffn = map(sem, ["t_x2T", "t_ffn"])
        a_xT, a_v, a_qT, a_k, a_exp = map(sem, ["a_xT", "a_v", "a_qT", "a_k", "a_exp"])
        a_pT, a_oT, a_x1T, a_cexp = map(sem, ["a_pT", "a_oT", "a_x1T", "a_cexp"])
        a_cpT, a_coT, a_x2T, a_cq, a_ck, a_cv = map(sem, ["a_cpT", "a_coT", "a_x2T", "a_cq", "a_ck", "a_cv"])
        d_stats = [sem(f"d_stats{i}") for i in range(3)]
        d_mv = [sem(f"d_mv{i}") for i in range(3)]
        d_xlo, d_q, d_k, d_masked, d_max, d_sub, d_sum, d_inv, d_x1 = map(
            sem, ["d_xlo", "d_q", "d_k", "d_masked", "d_max", "d_sub", "d_sum", "d_inv", "d_x1"])
        d_cmax, d_csub, d_csum, d_cinv, d_x2 = map(
            sem, ["d_cmax", "d_csub", "d_csum", "d_cinv", "d_x2"])
        d_ffn, d_clipped = map(sem, ["d_ffn", "d_clipped"])
        g_veps = [sem(f"g_veps{i}") for i in range(3)]
        g_rstd = [sem(f"g_rstd{i}") for i in range(3)]
        g_xn, g_x1n, g_x2n, g_xres, g_q, g_k, g_x1bo, g_probs, g_cprobs, g_biased, g_y = map(
            sem, ["g_xn", "g_x1n", "g_x2n", "g_xres", "g_q", "g_k", "g_x1bo", "g_probs", "g_cprobs", "g_biased",
                  "g_y"])

        class Tile:

            def __init__(self, base, off):
                self.base, self.off = base, off
                self.looped = not isinstance(base, int)
                self.n = base + off
                self.par = (off if self.looped else base + off) % 2
                self.landed = (self.n - self.par) * 8 + 16

            def exists(self, before=0):
                return self.looped or 0 <= self.n - before < NT

        class Step:

            def __init__(self, base, off=0):
                self.base, self.off = base, off

            def tile(self, stage):
                return Tile(self.base, self.off + 1 - stage)

        def run(eng, body):
            for s in range(1, LOOP_FROM):
                body(Step(s))
            with eng.Fori(LOOP_FROM, LOOP_TO - 1, 2) as s:
                body(Step(s, 0))
                body(Step(s, 1))
            for s in range(LOOP_TO, LAST_STEP + 1):
                body(Step(s))

        PROBS_T, C_PROBS_T, V = range(3)
        in_slot0 = [(3, a_pT), (5, a_cpT), (1, a_v)]
        probs_t_psum = c_probs_t_psum = v_psum = slot[0]
        Q_T, SCORES, ATTEND, K_T = range(4)
        in_slot1 = [(2, a_qT), (2, d_masked), (3, a_oT), (1, a_k)]
        q_t_psum = scores_psum = attend_psum = k_t_psum = slot[1]
        K, Q, C_SCORES = range(3)
        in_slot2 = [(1, d_k), (1, d_q), (4, d_csub)]
        k_psum = q_psum = c_scores_psum = slot[2]
        OUT, FFN, C_ATTEND, C_OUT = range(4)
        in_bank0 = [(4, d_x1), (6, d_ffn), (5, a_coT), (5, d_x2)]
        out_psum = ffn_psum = c_attend_psum = c_out_psum = bank[0]
        X_T, X2_T, C_K, X1_T, C_Q, C_V = range(6)
        in_bank1 = [(1, d_xlo), (6, a_x2T), (4, a_ck), (4, a_x1T), (4, a_cq), (4, a_cv)]
        x_psum = x2_psum = c_k_psum = x1_psum = c_q_psum = c_v_psum = bank[1]

        def read_out(held, me, s):
            for back in range(1, (LAST_STAGE + 1) * len(held)):
                stage, read = held[(me - back) % len(held)]
                tile = Tile(s.base, s.off + 1 - stage - (len(held) - 1 - me + back) // len(held))
                if tile.exists():
                    return read, tile.n + 1
            return ident_loaded, 16

        weight_loads = [(1, w_k), (0, w_q), (2, w_v)]
        rest_loads = [
            (mask[:], mask_in), (fw_raw[:], f_w), (wo[:], w_o), (cwq[:], c_wq), (cwk[:], c_wk), (cwv[:], c_wv),
            (cwo[:], c_wo), (cbq[:], c_bq), (cbk[:], c_bk), (cbv[:], c_bv), (cbo[:], c_bo.broadcast_to([P, D])),
            (fscale[:], f_scale.broadcast_to([P, D])), (fbias[:], f_bias.broadcast_to([P, D])),
            (jmask[:], group_in),
        ]
        ALL_REST = 16 * len(rest_loads)

        def halves(a):
            return [a[:, i * BANK:(i + 1) * BANK] for i in range(F // BANK)]

        def squares(a):
            return [a[:, i * P:(i + 1) * P] for i in range(F // P)]

        def seq(b):
            return slice(b * SEQ, (b + 1) * SEQ)

        def for_heads(a, width):
            return a[:].unsqueeze(2).broadcast_to([P, H, width])

        block = ctx.enter_context(nc.Block())

        @block.sync
        def _(sp):
            def load_x(t):
                if t.exists():
                    if t.exists(2):
                        sp.wait_ge(g_xres, t.n - 1)
                        sp.wait_ge(g_xn, t.n - 1)
                    sp.dma_start(x_in[t.par][:], x[bass.ds(t.n * P, P), :]).then_inc(x_loaded[t.par], 16)

            load_x(Tile(0, 0))
            sp.dma_start(ident[:], ident_in).then_inc(ident_loaded, 16)
            for i, src in weight_loads:
                sp.dma_start(w_qkv[i][:], src).then_inc(w_in[i], 16)
            sp.dma_start(rope_c[:], rope_in[0]).then_inc(rope_loaded, 16)
            sp.dma_start(rope_s[:], rope_in[1]).then_inc(rope_loaded, 16)

            def step(s):
                t = s.tile(3)
                if t.exists():
                    if t.exists(2):
                        sp.wait_ge(t_cv, t.n - 1)
                    sp.dma_start(ctxT[t.par][:], ctx_t[:, bass.ds(t.n * P, P)]).then_inc(ctx_loaded[t.par], 16)
                load_x(Tile(s.base, s.off + 2))
                t = s.tile(6)
                if t.exists():
                    sp.wait_ge(g_y, t.n + 1)
                    sp.dma_start(out[bass.ds(t.n * P, P), :], y[t.par][:]).then_inc(y_stored[t.par], 16)

            step(Step(-1))
            for i in range(3):
                sp.wait_ge(w_in[i], 16)
            for dst, src in rest_loads:
                sp.dma_start(dst, src).then_inc(rest_in, 16)
            step(Step(0))
            run(sp, step)
            for t in (Tile(NT - 2, 0), Tile(NT - 1, 0)):
                sp.wait_ge(y_stored[t.par], t.landed)

        @block.tensor
        def _(pe):
            mm, transpose = nc.tensor.matmul, nc.tensor.transpose
            pe.wait_ge(ident_loaded, 16)

            def context_v(t):
                for b in range(NB):
                    for par in range(2):
                        last = mm(c_v_psum[seq(par), b * (D // 2):(b + 1) * (D // 2)], ctxT[t.par][:, seq(b)],
                                  cwv[:, par, :], start=True, stop=True, skip_group_check=True)
                return last

            def scores():
                for pair, cols in enumerate(squares(scores_psum)):
                    for b in range(NB):
                        last = mm(cols[seq(b), :], qT[:, pair, seq(b)],
                                  k_bd[:, pair, b, :, :].rearrange("p a k -> p (a k)"),
                                  start=True, stop=True, skip_group_check=True)
                return last

            def projection(psum, which):
                for cols, hi, lo in zip(halves(psum), halves(w_hi[which]), halves(w_lo[which])):
                    mm(cols, xnT_hi[:], hi, start=True, stop=False)
                    mm(cols, xnT_hi[:], lo, start=False, stop=False)
                    last = mm(cols, xnT_lo[:], hi, start=False, stop=True)
                return last

            def cross_scores():
                width = GROUP * SEQ
                for g in range(GROUP):
                    for b in range(NB):
                        last = mm(c_scores_psum[seq(b), g * width:(g + 1) * width], cq_g[:, g, seq(b)],
                                  ck_j[:, :, seq(b)], start=True, stop=True, skip_group_check=True)
                return last

            def attend(t):
                for pair, cols in enumerate(squares(attend_psum)):
                    for par in range(2):
                        head = 2 * pair + par
                        last = mm(cols[seq(par), :], v[t.par][:, head * HD:(head + 1) * HD],
                                  p_bd[:, pair, par, :, :].rearrange("p b q -> p (b q)"),
                                  start=True, stop=True, skip_group_check=True)
                return last

            def cross_attend():
                for b in range(NB):
                    for k in range(2):
                        for g in range(GROUP):
                            pair = 2 * g + k
                            last = mm(c_attend_psum[g * QUAD:(g + 1) * QUAD, seq(b)], cv_bd[:, b, pair, :],
                                      cpT[:, pair, seq(b)], start=k == 0, stop=k == 1, skip_group_check=True)
                return last

            def out_proj():
                for pair in range(PAIRS):
                    last = mm(out_psum[:, 0:D], oT[:, pair, :], wo[:, pair, :],
                              start=pair == 0, stop=pair == PAIRS - 1)
                return last

            def transposes(psum, src):
                for dst, square in zip(squares(psum), squares(src)):
                    last = transpose(dst, square, ident[:])
                return last

            def step(s):
                t0, t1, t2, t3, t4, t5, t6 = (s.tile(stage) for stage in range(7))
                if t1.exists():
                    pe.wait_ge(*read_out(in_bank1, X_T, s))
                    pe.wait_ge(g_xn, t1.n + 1)
                    transpose(x_psum[:, 0:P], xn[:], ident[:]).then_inc(t_xT, 1)
                if t4.exists():
                    pe.wait_ge(*read_out(in_bank0, OUT, s))
                    pe.wait_ge(a_oT, t4.n + 1)
                    out_proj().then_inc(t_out, 1)
                if t2.exists():
                    pe.wait_ge(*read_out(in_slot1, Q_T, s))
                    pe.wait_ge(g_q, t2.n + 1)
                    transposes(q_t_psum, q_rot[:]).then_inc(t_qT, 1)
                if t6.exists():
                    pe.wait_ge(*read_out(in_bank1, X2_T, s))
                    pe.wait_ge(g_x2n, t6.n + 1)
                    transpose(x2_psum[:, 0:P], x2n[:], ident[:]).then_inc(t_x2T, 1)
                if t1.exists():
                    pe.wait_ge(*read_out(in_slot2, K, s))
                    pe.wait_ge(d_xlo, t1.n + 1)
                    if not t1.exists(1):
                        pe.wait_ge(dve_setup, 1)
                    projection(k_psum, 1).then_inc(t_k, 1)
                if t6.exists():
                    pe.wait_ge(*read_out(in_bank0, FFN, s))
                    pe.wait_ge(a_x2T, t6.n + 1)
                    mm(ffn_psum[:, 0:D], x2nT[:], fw[:], start=True, stop=True).then_inc(t_ffn, 1)
                if t4.exists():
                    pe.wait_ge(*read_out(in_bank1, C_K, s))
                    pe.wait_ge(ctx_loaded[t4.par], t4.landed)
                    mm(c_k_psum[:, 0:P], cwk[:], ctxT[t4.par][:], start=True, stop=True).then_inc(t_ck, 1)
                if t3.exists():
                    pe.wait_ge(*read_out(in_slot0, PROBS_T, s))
                    pe.wait_ge(g_probs, t3.n + 1)
                    transposes(probs_t_psum, probs[:].rearrange("p h k -> p (h k)")).then_inc(t_pT, 1)
                if t2.exists():
                    pe.wait_ge(*read_out(in_slot1, SCORES, s))
                    pe.wait_ge(a_qT, t2.n + 1)
                    pe.wait_ge(a_k, t2.n + 1)
                    scores().then_inc(t_s, 1)
                if t4.exists():
                    pe.wait_ge(*read_out(in_bank1, X1_T, s))
                    pe.wait_ge(g_x1n, t4.n + 1)
                    transpose(x1_psum[:, 0:P], x1n[:], ident[:]).then_inc(t_x1T, 1)
                if t1.exists():
                    pe.wait_ge(*read_out(in_slot2, Q, s))
                    pe.wait_ge(d_xlo, t1.n + 1)
                    if not t1.exists(1):
                        pe.wait_ge(dve_setup, 2)
                    projection(q_psum, 0).then_inc(t_q, 1)
                if t5.exists():
                    pe.wait_ge(*read_out(in_slot0, C_PROBS_T, s))
                    pe.wait_ge(g_cprobs, t5.n + 1)
                    transposes(c_probs_t_psum, cprobs[:].rearrange("p h k -> p (h k)")).then_inc(t_cpT, 1)
                if t4.exists():
                    pe.wait_ge(*read_out(in_bank1, C_Q, s))
                    pe.wait_ge(a_x1T, t4.n + 1)
                    mm(c_q_psum[:, 0:P], cwq[:], x1nT[:], start=True, stop=True).then_inc(t_cq, 1)
                if t3.exists():
                    pe.wait_ge(*read_out(in_slot1, ATTEND, s))
                    pe.wait_ge(a_v, t3.n + 1)
                    pe.wait_ge(a_pT, t3.n + 1)
                    attend(t3).then_inc(t_o, 1)
                if t4.exists():
                    pe.wait_ge(*read_out(in_slot2, C_SCORES, s))
                    pe.wait_ge(a_ck, t4.n + 1)
                    pe.wait_ge(a_cq, t4.n + 1)
                    cross_scores().then_inc(t_cs, 1)
                if t5.exists():
                    pe.wait_ge(*read_out(in_bank0, C_ATTEND, s))
                    pe.wait_ge(a_cv, t5.n + 1)
                    pe.wait_ge(a_cpT, t5.n + 1)
                    cross_attend().then_inc(t_co, 1)
                if t4.exists():
                    pe.wait_ge(*read_out(in_bank1, C_V, s))
                    pe.wait_ge(ctx_loaded[t4.par], t4.landed)
                    context_v(t4).then_inc(t_cv, 1)
                if t1.exists():
                    pe.wait_ge(*read_out(in_slot1, K_T, s))
                    pe.wait_ge(g_k, t1.n + 1)
                    transposes(k_t_psum, k_rot[:]).then_inc(t_kT, 1)
                if t5.exists():
                    pe.wait_ge(*read_out(in_bank0, C_OUT, s))
                    pe.wait_ge(a_coT, t5.n + 1)
                    mm(c_out_psum[:, 0:D], coT[:], cwo[:], start=True, stop=True).then_inc(t_cout, 1)
                if t1.exists():
                    pe.wait_ge(*read_out(in_slot0, V, s))
                    pe.wait_ge(d_xlo, t1.n + 1)
                    if not t1.exists(1):
                        pe.wait_ge(dve_setup, 3)
                    projection(v_psum, 2).then_inc(t_v, 1)

            step(Step(-1))
            step(Step(0))
            pe.wait_ge(rest_in, ALL_REST)
            pe.wait_ge(dve_setup, 4)
            pe.wait_ge(pool_setup, 2)
            run(pe, step)

        @block.scalar
        def _(act):
            copy = nc.scalar.copy
            for i, _ in weight_loads:
                act.wait_ge(w_in[i], 16)
                copy(w_hi[i][:], w_qkv[i][:]).then_inc(act_setup, 1)

            def wide(a):
                return a[:].rearrange("p r t -> p (r t)")

            def heads_and_seqs(a):
                return a[:].rearrange("p (r b q) -> p r b q", b=NB, q=SEQ)

            def diagonal(blocks, par):
                first = blocks[seq(par), 0, 0, par * CHD:(par + 1) * CHD]
                return bass.AP(first.tensor, first.offset,
                               [first.ap[0], [2 * QUAD, NB * GROUP], [QUAD + 2 * CHD, 2], [1, CHD]])

            def step(s):
                t0, t1, t2, t3, t4, t5, t6 = (s.tile(stage) for stage in range(7))
                if t5.exists():
                    act.wait_ge(t_cv, t5.n + 1)
                    if t5.exists(1):
                        act.wait_ge(t_co, t5.n)
                    for par in range(2):
                        last = copy(diagonal(cv_bd, par), c_v_psum[seq(par), 0:D].rearrange("p (q k d) -> p q k d", k=2, d=CHD))
                    last.then_inc(a_cv, 1)
                if t3.exists():
                    act.wait_ge(d_sub, t3.n + 1)
                    nc.scalar.activation(probs[:], probs[:], ACT.Exp, scale=float(HD) ** -0.5).then_inc(a_exp, 1)
                if t2.exists():
                    act.wait_ge(t_kT, t2.n + 1)
                    if t2.exists(1):
                        act.wait_ge(t_s, t2.n)
                    for par in range(2):
                        last = copy(k_bd[seq(par), :, :, par, :].rearrange("p r b k -> p (r b) k"),
                                    k_t_psum[seq(par), :].rearrange("p (r k) -> p r k", k=SEQ))
                    last.then_inc(a_k, 1)
                if t1.exists():
                    act.wait_ge(t_xT, t1.n + 1)
                    if t1.exists(1):
                        act.wait_ge(t_v, t1.n)
                    copy(xnT_hi[:], x_psum[:, 0:P]).then_inc(a_xT, 1)
                if t2.exists():
                    act.wait_ge(t_v, t2.n + 1)
                    if t2.exists(2):
                        act.wait_ge(t_o, t2.n - 1)
                    copy(v[t2.par][:], v_psum[:]).then_inc(a_v, 1)
                if t5.exists():
                    act.wait_ge(d_csub, t5.n + 1)
                    nc.scalar.activation(cprobs[:], cprobs[:], ACT.Exp, scale=float(CHD) ** -0.5).then_inc(a_cexp, 1)
                if t6.exists():
                    act.wait_ge(t_x2T, t6.n + 1)
                    if t6.exists(1):
                        act.wait_ge(t_ffn, t6.n)
                    copy(x2nT[:], x2_psum[:, 0:P]).then_inc(a_x2T, 1)
                if t2.exists():
                    act.wait_ge(t_qT, t2.n + 1)
                    if t2.exists(1):
                        act.wait_ge(t_s, t2.n)
                    copy(wide(qT), q_t_psum[:]).then_inc(a_qT, 1)
                if t4.exists():
                    act.wait_ge(t_ck, t4.n + 1)
                    if t4.exists(1):
                        act.wait_ge(t_cs, t4.n)
                    for j in range(GROUP):
                        last = nc.scalar.activation(ck_j[:, j, :], c_k_psum[:, 0:P], ACT.Identity, bias=cbk_j[:, j:j + 1],
                                                    scale=jmask[:, j:j + 1])
                    last.then_inc(a_ck, 1)
                if t3.exists():
                    act.wait_ge(t_pT, t3.n + 1)
                    if t3.exists(1):
                        act.wait_ge(t_o, t3.n)
                    for b in range(NB):
                        for par in range(2):
                            last = copy(p_bd[seq(b), :, par, b, :], heads_and_seqs(probs_t_psum)[seq(par), :, b, :])
                    last.then_inc(a_pT, 1)
                if t4.exists():
                    act.wait_ge(t_x1T, t4.n + 1)
                    if t4.exists(1):
                        act.wait_ge(t_cq, t4.n)
                    copy(x1nT[:], x1_psum[:, 0:P]).then_inc(a_x1T, 1)
                if t4.exists():
                    act.wait_ge(t_cq, t4.n + 1)
                    if t4.exists(1):
                        act.wait_ge(t_cs, t4.n)
                    for g in range(GROUP):
                        rows = slice(g * QUAD, (g + 1) * QUAD)
                        last = nc.scalar.activation(cq_g[rows, g, :], c_q_psum[rows, 0:P], ACT.Identity, bias=cbq[rows])
                    last.then_inc(a_cq, 1)
                if t5.exists():
                    act.wait_ge(t_cpT, t5.n + 1)
                    if t5.exists(1):
                        act.wait_ge(t_co, t5.n)
                    copy(wide(cpT), c_probs_t_psum[:]).then_inc(a_cpT, 1)
                if t3.exists():
                    act.wait_ge(t_o, t3.n + 1)
                    if t3.exists(1):
                        act.wait_ge(t_out, t3.n)
                    copy(wide(oT), attend_psum[:]).then_inc(a_oT, 1)
                if t5.exists():
                    act.wait_ge(t_co, t5.n + 1)
                    if t5.exists(1):
                        act.wait_ge(t_cout, t5.n)
                    nc.scalar.activation(coT[:], c_attend_psum[:, 0:P], ACT.Identity, bias=cbv[:]).then_inc(a_coT, 1)

            step(Step(-1))
            act.wait_ge(pool_setup, 2)
            step(Step(0))
            act.wait_ge(rest_in, ALL_REST)
            act.wait_ge(dve_setup, 4)
            run(act, step)

        @block.vector
        def _(dve):
            tt = nc.vector.tensor_tensor

            def mean_and_variance(t, k, src):
                nc.vector.bn_stats(stats[k][:], src).then_inc(d_stats[k], 1)
                dve.wait_ge(d_stats[k], t.n + 1)
                tt(after_stats[:], eps[:], eps[:], ALU.add)
                nc.vector.bn_aggr(mv[k][:], stats[k][:]).then_inc(d_mv[k], 1)

            def by_head(a, width):
                return a.rearrange("p (h d) -> p h d", d=width)

            def rope_products(q_or_k, with_cos, with_sin):
                v = by_head(q_or_k, HD)
                tt(by_head(with_cos[:], HD), v, rope_c[:].unsqueeze(1).broadcast_to([P, H, HD]), ALU.mult)
                return tt(by_head(with_sin[:], HD), v, rope_s[:].unsqueeze(1).broadcast_to([P, H, HD]), ALU.mult)

            def step(s):
                t0, t1, t2, t3, t4, t5, t6 = (s.tile(stage) for stage in range(7))
                if t3.exists():
                    dve.wait_ge(d_masked, t3.n + 1)
                    nc.vector.tensor_reduce(pmax[:], probs[:], AX_X, ALU.max).then_inc(d_max, 1)
                    dve.wait_ge(d_max, t3.n + 1)
                    tt(probs[:], probs[:], for_heads(pmax, SEQ), ALU.subtract).then_inc(d_sub, 1)
                if t5.exists():
                    dve.wait_ge(t_cs, t5.n + 1)
                    nc.vector.tensor_reduce(cmax[:], by_head(c_scores_psum[:], SEQ), AX_X, ALU.max).then_inc(d_cmax, 1)
                    dve.wait_ge(d_cmax, t5.n + 1)
                    if t5.exists(1):
                        dve.wait_ge(t_cpT, t5.n)
                    tt(cprobs[:], by_head(c_scores_psum[:], SEQ), for_heads(cmax, SEQ), ALU.subtract).then_inc(d_csub, 1)
                if t6.exists():
                    dve.wait_ge(t_cout, t6.n + 1)
                    dve.wait_ge(g_x1bo, t6.n + 1)
                    if t6.exists(1):
                        dve.wait_ge(g_x2n, t6.n)
                    if t6.exists(2):
                        dve.wait_ge(g_y, t6.n - 1)
                    tt(x2[t6.par][:], c_out_psum[:, 0:D], x1_bo[t6.par][:], ALU.add).then_inc(d_x2, 1)
                    dve.wait_ge(d_x2, t6.n + 1)
                    mean_and_variance(t6, 2, x2[t6.par][:])
                if t3.exists():
                    dve.wait_ge(a_exp, t3.n + 1)
                    if t3.exists(1):
                        dve.wait_ge(g_probs, t3.n)
                    nc.vector.tensor_reduce(psum_[:], probs[:], AX_X, ALU.add).then_inc(d_sum, 1)
                    dve.wait_ge(d_sum, t3.n + 1)
                    nc.vector.reciprocal(pinv[:], psum_[:]).then_inc(d_inv, 1)
                if t1.exists():
                    dve.wait_ge(a_xT, t1.n + 1)
                    if t1.exists(1):
                        dve.wait_ge(t_v, t1.n)
                    tt(xnT_lo[:], x_psum[:, 0:P], xnT_hi[:].bitcast(F32), ALU.subtract).then_inc(d_xlo, 1)
                if t4.exists():
                    dve.wait_ge(t_out, t4.n + 1)
                    dve.wait_ge(g_xres, t4.n + 1)
                    if t4.exists(1):
                        dve.wait_ge(g_x1bo, t4.n)
                    tt(x1[:], out_psum[:, 0:D], x_res[t4.par][:], ALU.add).then_inc(d_x1, 1)
                    dve.wait_ge(d_x1, t4.n + 1)
                    mean_and_variance(t4, 1, x1[:])
                if t5.exists():
                    dve.wait_ge(a_cexp, t5.n + 1)
                    if t5.exists(1):
                        dve.wait_ge(g_cprobs, t5.n)
                    nc.vector.tensor_reduce(csum[:], cprobs[:], AX_X, ALU.add).then_inc(d_csum, 1)
                    dve.wait_ge(d_csum, t5.n + 1)
                    nc.vector.reciprocal(cinv[:], csum[:]).then_inc(d_cinv, 1)
                if t1.exists():
                    dve.wait_ge(t_k, t1.n + 1)
                    if t1.exists(1):
                        dve.wait_ge(g_k, t1.n)
                    rope_products(k_psum[:], k_cos, k_sin).then_inc(d_k, 1)
                if t6.exists():
                    dve.wait_ge(t_ffn, t6.n + 1)
                    if t6.exists(1):
                        dve.wait_ge(g_biased, t6.n)
                    tt(f_scaled[:], ffn_psum[:, 0:D], fscale[:], ALU.mult).then_inc(d_ffn, 1)
                if t0.exists():
                    if t0.exists(1):
                        dve.wait_ge(x_loaded[t0.par], t0.landed)
                        dve.wait_ge(g_xn, t0.n)
                        mean_and_variance(t0, 0, x_in[t0.par][:])
                if t2.exists():
                    dve.wait_ge(t_s, t2.n + 1)
                    if t2.exists(1):
                        dve.wait_ge(t_pT, t2.n)
                    tt(probs[:], by_head(scores_psum[:], SEQ), mask[:].unsqueeze(1).broadcast_to([P, H, SEQ]),
                       ALU.add).then_inc(d_masked, 1)
                if t6.exists():
                    dve.wait_ge(g_biased, t6.n + 1)
                    if t6.exists(1):
                        dve.wait_ge(g_y, t6.n)
                    nc.vector.tensor_scalar(f_clipped[:], f_biased[:], CLIP, -CLIP, ALU.min, ALU.max).then_inc(d_clipped, 1)
                if t1.exists():
                    dve.wait_ge(t_q, t1.n + 1)
                    if t1.exists(1):
                        dve.wait_ge(g_q, t1.n)
                    rope_products(q_psum[:], q_cos, q_sin).then_inc(d_q, 1)

            dve.wait_ge(pool_setup, 1)
            dve.wait_ge(x_loaded[0], 16)
            mean_and_variance(Tile(0, 0), 0, x_in[0][:])
            for ready, (i, _) in enumerate(weight_loads):
                dve.wait_ge(w_in[i], 16)
                dve.wait_ge(act_setup, ready + 1)
                tt(w_lo[i][:], w_qkv[i][:], w_hi[i][:].bitcast(F32), ALU.subtract).then_inc(dve_setup, 1)
            dve.wait_ge(rope_loaded, 2 * 16)
            step(Step(-1))
            step(Step(0))
            dve.wait_ge(rest_in, ALL_REST)
            nc.vector.tensor_scalar(fw[:], fw_raw[:], 0.0, 2.0, ALU.is_ge, ALU.mult).then_inc(fw_doubled, 1)
            tt(cbk_j[:], cbk[:].broadcast_to([P, GROUP]), jmask[:], ALU.mult)
            dve.wait_ge(fw_doubled, 1)
            nc.vector.tensor_scalar(fw[:], fw[:], 1.0, None, ALU.subtract).then_inc(dve_setup, 1)
            run(dve, step)

        @block.gpsimd
        def _(pool):
            tt = nc.gpsimd.tensor_tensor

            def centre_and_root(t, k, src):
                pool.wait_ge(d_mv[k], t.n + 1)
                tt(veps[k][:], mv[k][:, 1:2], eps[:], ALU.add).then_inc(g_veps[k], 1)
                tt(centred[k][:], src, mv[k][:, 0:1].broadcast_to([P, D]), ALU.subtract)
                pool.wait_ge(g_veps[k], t.n + 1)
                tt(rstd[k][:], veps[k][:], neg_half[:], ALU.pow).then_inc(g_rstd[k], 1)
                pool.wait_ge(g_rstd[k], t.n + 1)

            def rope_sum(dst, with_cos, with_sin):
                d, c, s = (a[:].rearrange("p (h a i) -> p h a i", a=2, i=HD // 2) for a in (dst, with_cos, with_sin))
                tt(d[:, :, 0, :], c[:, :, 0, :], s[:, :, 1, :], ALU.add)
                return tt(d[:, :, 1, :], c[:, :, 1, :], s[:, :, 0, :], ALU.add)

            def scaled(dst, k):
                return tt(dst[:], centred[k][:], rstd[k][:].broadcast_to([P, D]), ALU.mult)

            def step(s):
                t0, t1, t2, t3, t4, t5, t6 = (s.tile(stage) for stage in range(7))
                if t2.exists():
                    pool.wait_ge(d_q, t2.n + 1)
                    if t2.exists(1):
                        pool.wait_ge(t_qT, t2.n)
                    rope_sum(q_rot, q_cos, q_sin).then_inc(g_q, 1)
                if t6.exists():
                    centre_and_root(t6, 2, x2[t6.par][:])
                    if t6.exists(1):
                        pool.wait_ge(t_x2T, t6.n)
                    scaled(x2n, 2).then_inc(g_x2n, 1)
                if t3.exists():
                    pool.wait_ge(d_inv, t3.n + 1)
                    tt(probs[:], probs[:], for_heads(pinv, SEQ), ALU.mult).then_inc(g_probs, 1)
                if t2.exists():
                    pool.wait_ge(x_loaded[t2.par], t2.landed)
                    if t2.exists(2):
                        pool.wait_ge(d_x1, t2.n - 1)
                    tt(x_res[t2.par][:], x_in[t2.par][:], zero[:].broadcast_to([P, D]), ALU.add).then_inc(g_xres, 1)
                if t4.exists():
                    centre_and_root(t4, 1, x1[:])
                    if t4.exists(1):
                        pool.wait_ge(t_x1T, t4.n)
                    scaled(x1n, 1).then_inc(g_x1n, 1)
                    if t4.exists(2):
                        pool.wait_ge(d_x2, t4.n - 1)
                    tt(x1_bo[t4.par][:], x1[:], cbo[:], ALU.add).then_inc(g_x1bo, 1)
                if t5.exists():
                    pool.wait_ge(d_cinv, t5.n + 1)
                    tt(cprobs[:], cprobs[:], for_heads(cinv, SEQ), ALU.mult).then_inc(g_cprobs, 1)
                if t6.exists():
                    pool.wait_ge(d_ffn, t6.n + 1)
                    if t6.exists(1):
                        pool.wait_ge(d_clipped, t6.n)
                    tt(f_biased[:], f_scaled[:], fbias[:], ALU.add).then_inc(g_biased, 1)
                if t6.exists():
                    pool.wait_ge(d_clipped, t6.n + 1)
                    if t6.exists(2):
                        pool.wait_ge(y_stored[t6.par], t6.landed - 16)
                    tt(y[t6.par][:], f_clipped[:], x2[t6.par][:], ALU.add).then_inc(g_y, 1)
                if t0.exists():
                    centre_and_root(t0, 0, x_in[t0.par][:])
                    if t0.exists(1):
                        pool.wait_ge(t_xT, t0.n)
                    scaled(xn, 0).then_inc(g_xn, 1)
                if t1.exists():
                    pool.wait_ge(d_k, t1.n + 1)
                    if t1.exists(1):
                        pool.wait_ge(t_kT, t1.n)
                    rope_sum(k_rot, k_cos, k_sin).then_inc(g_k, 1)

            nc.gpsimd.memset(eps[:], EPS)
            nc.gpsimd.memset(zero[:], 0.0)
            nc.gpsimd.memset(neg_half[:], -0.5).then_inc(pool_setup, 1)
            pool.wait_ge(pool_setup, 1)
            step(Step(-1))
            nc.gpsimd.memset(k_bd[:], 0.0)
            nc.gpsimd.memset(p_bd[:], 0.0)
            nc.gpsimd.memset(cq_g[:], 0.0)
            nc.gpsimd.memset(cv_bd[:], 0.0).then_inc(pool_setup, 1)
            step(Step(0))
            pool.wait_ge(rest_in, ALL_REST)
            run(pool, step)


def _constants():
    pos = np.arange(P) % SEQ
    freqs = (1.0 / 10000.0 ** (np.arange(0, HD, 2, dtype=np.float32) / np.float32(HD))).astype(np.float32)
    angles = (np.arange(SEQ, dtype=np.float32)[:, None] * freqs[None, :]).astype(np.float32)[pos]
    cos, sin = np.cos(angles).astype(np.float32), np.sin(angles).astype(np.float32)
    rope = np.stack([np.concatenate([cos, cos], 1), np.concatenate([sin, -sin], 1)])
    mask = np.where(np.arange(SEQ)[None, :] <= pos[:, None], 0.0, MASKED).astype(np.float32)
    head = np.arange(P) // CHD
    groups = head[:, None] % GROUP == np.arange(GROUP)
    return np.eye(P, dtype=np.float32), mask, rope.astype(np.float32), groups.astype(np.float32)


def kernel(x, ctx_1024, L0_attn_W_qkv, L0_attn_W_out, L0_xattn_Wq, L0_xattn_bq, L0_xattn_Wk, L0_xattn_bk,
           L0_xattn_Wv, L0_xattn_bv, L0_xattn_Wo, L0_xattn_bo, L0_ffn_weights, L0_ffn_scale, L0_ffn_bias):
    import concourse.bacc as _bacc
    from concourse.bass_utils import run_bass_kernel_spmd as _run

    a = np.asarray
    B, S, _ = x.shape
    wqkv = a(L0_attn_W_qkv).reshape(D, 3, H, HD)
    qk = wqkv[:, :2].reshape(D, 2, H, HD // 2, 2).transpose(1, 0, 2, 4, 3).reshape(2, D, F)
    wv = wqkv[:, 2].reshape(D, F)
    wo = a(L0_attn_W_out).reshape(PAIRS, 2 * HD, D).transpose(1, 0, 2)
    cwv = a(L0_xattn_Wv).T.reshape(D, PAIRS, 2, CHD).transpose(0, 2, 1, 3).reshape(D, 2, D // 2)
    ident, mask, rope, groups = _constants()
    arrays = {
        "x": a(x).reshape(B * S, D), "ctx_t": a(ctx_1024).reshape(B * S, D).T, "w_q": qk[0], "w_k": qk[1],
        "w_v": wv, "w_o": wo, "c_wq": a(L0_xattn_Wq).T, "c_wk": a(L0_xattn_Wk).T, "c_wv": cwv,
        "c_wo": a(L0_xattn_Wo).T, "c_bq": a(L0_xattn_bq).reshape(D, 1), "c_bk": a(L0_xattn_bk).reshape(D, 1),
        "c_bv": a(L0_xattn_bv).reshape(D, 1), "c_bo": a(L0_xattn_bo).reshape(1, D), "f_w": a(L0_ffn_weights).T,
        "f_scale": a(L0_ffn_scale).reshape(1, D), "f_bias": a(L0_ffn_bias).reshape(1, D),
        "ident": ident, "mask": mask, "rope": rope, "groups": groups,
    }
    arrays = {f"in_{k}": np.ascontiguousarray(v) for k, v in arrays.items()}
    nc = _bacc.Bacc("TRN2", target_bir_lowering=False, num_devices=1)
    args = [nc.dram_tensor(k, v.shape, mybir.dt.from_np(v.dtype), kind="ExternalInput").ap()
            for k, v in arrays.items()]
    args.append(nc.dram_tensor("out_y", (B * S, D), F32, kind="ExternalOutput").ap())
    decoder_layer(nc, *args)
    r = _run(nc, [arrays], core_ids=[0])
    return r.results[0]["out_y"].reshape(B, S, D)
```
